# Optimizing a Trainium2 kernel written in Bass

```python
import numpy as np
import jax
import jax.numpy as jnp

def _softmax(x, axis=-1):
    return jax.nn.softmax(x, axis=axis)

def _gelu(x):
    return jax.nn.gelu(x, approximate=True)

def _silu(x):
    return jax.nn.silu(x)

def _sigmoid(x):
    return jax.nn.sigmoid(x)

def _layernorm(x, axis=-1, eps=1e-05):
    m = jnp.mean(x, axis=axis, keepdims=True)
    v = jnp.var(x, axis=axis, keepdims=True)
    return (x - m) / jnp.sqrt(v + eps)

def _scatter_add(tgt, idx, src, axis=0):
    return tgt.at[idx].add(src)

def _segment_sum(src, seg, n):
    return jax.ops.segment_sum(src, seg, n)
kernel_name = 'mk_adj_ffn_d1_adj_r2_ae7d67'

def setup_inputs(seed: int=0):
    np.random.seed(seed)
    _w = jnp.asarray

    def _rec_inputs():
        import jax
        import jax.numpy as jnp
        _gk = jax.random.key(seed)
        x = -0.0002928 + 1 * jax.random.normal(jax.random.fold_in(_gk, 1), (16, 512, 128), jnp.float32)
        _a = jax.random.bernoulli(jax.random.fold_in(_gk, 2), 0.00390625, (16, 512, 512))
        _a = jnp.logical_or(_a, jnp.swapaxes(_a, -1, -2))
        _a = jnp.logical_or(_a, jnp.eye(512, dtype=bool))
        adj = _a.astype(jnp.int32)
        return (x, adj)
    x, adj = _rec_inputs()

    def _L0_gnn_setup():
        import jax, jax.numpy as jnp
        import numpy as np
        key = jax.random.key(seed)
        k1, k2, k3, k4 = jax.random.split(key, 4)
        B, N, F, U = (8, 1024, 128, 128)
        x = jax.random.normal(k1, (B, N, F), dtype=jnp.float32)
        adj = jax.random.randint(k2, (B, N, N), 0, 2, dtype=jnp.int32)
        W_msg = jax.random.normal(k3, (F, U), dtype=jnp.float32) / np.sqrt(F)
        W_upd = jax.random.normal(k4, (F, U), dtype=jnp.float32) / np.sqrt(F)
        bias = jnp.zeros((U,), dtype=jnp.float32)
        return {'x': x, 'adj': adj, 'W_msg': W_msg, 'W_upd': W_upd, 'bias': bias}
    _L0_gnn_all = _L0_gnn_setup()
    _L0_gnn_in = {k: v for k, v in _L0_gnn_all.items() if k in ('W_msg', 'W_upd', 'bias')}
    del _L0_gnn_all

    def _L0_ffn_setup():
        import jax, jax.numpy as jnp
        import numpy as np
        TOP_K = 2
        LN_EPS = 1e-05
        key = jax.random.key(seed)
        ks = jax.random.split(key, 8)
        B, S, D, E, H = (16, 512, 128, 8, 512)
        x = jax.random.normal(ks[0], (B, S, D), dtype=jnp.float32)
        Wr = jax.random.normal(ks[1], (D, E), dtype=jnp.float32) * 0.1
        br = jnp.zeros((E,), dtype=jnp.float32)
        ln_g = jnp.ones((E, D), dtype=jnp.float32)
        ln_b = jnp.zeros((E, D), dtype=jnp.float32)
        W1 = jax.random.normal(ks[2], (E, D, H), dtype=jnp.float32) * (1.0 / np.sqrt(D))
        b1 = jnp.zeros((E, H), dtype=jnp.float32)
        W2 = jax.random.normal(ks[3], (E, H, D), dtype=jnp.float32) * (1.0 / np.sqrt(H))
        b2 = jnp.zeros((E, D), dtype=jnp.float32)
        return {'x': x, 'Wr': Wr, 'br': br, 'ln_g': ln_g, 'ln_b': ln_b, 'W1': W1, 'b1': b1, 'W2': W2, 'b2': b2}
    _L0_ffn_all = _L0_ffn_setup()
    _L0_ffn_in = {k: v for k, v in _L0_ffn_all.items() if k in ('Wr', 'br', 'ln_g', 'ln_b', 'W1', 'b1', 'W2', 'b2')}
    del _L0_ffn_all
    return {'x': x, 'adj': adj, 'L0_gnn_W_msg': _L0_gnn_in['W_msg'], 'L0_gnn_W_upd': _L0_gnn_in['W_upd'], 'L0_gnn_bias': _L0_gnn_in['bias'], 'L0_ffn_Wr': _L0_ffn_in['Wr'], 'L0_ffn_br': _L0_ffn_in['br'], 'L0_ffn_ln_g': _L0_ffn_in['ln_g'], 'L0_ffn_ln_b': _L0_ffn_in['ln_b'], 'L0_ffn_W1': _L0_ffn_in['W1'], 'L0_ffn_b1': _L0_ffn_in['b1'], 'L0_ffn_W2': _L0_ffn_in['W2'], 'L0_ffn_b2': _L0_ffn_in['b2']}

def reference(x, adj, L0_gnn_W_msg, L0_gnn_W_upd, L0_gnn_bias, L0_ffn_Wr, L0_ffn_br, L0_ffn_ln_g, L0_ffn_ln_b, L0_ffn_W1, L0_ffn_b1, L0_ffn_W2, L0_ffn_b2):
    import jax
    import jax.numpy as jnp

    def _L0_gnn_ref(x, adj, W_msg, W_upd, bias):
        import jax, jax.numpy as jnp
        import numpy as np
        a = adj.astype(x.dtype)
        h = jnp.einsum('bnf,fu->bnu', x, W_msg)
        msg_sum = jnp.einsum('bij,biu->bju', a, h)
        deg = jnp.sum(a, axis=1)
        messages = jnp.where(deg[..., None] > 0, msg_sum / jnp.maximum(deg, 1.0)[..., None], 0.0)
        out = jnp.einsum('bnf,fu->bnu', x, W_upd) + messages + bias
        return jax.nn.relu(out)

    def _L0_ffn_ref(x, Wr, br, ln_g, ln_b, W1, b1, W2, b2):
        import jax, jax.numpy as jnp
        import numpy as np
        TOP_K = 2
        LN_EPS = 1e-05
        B, S, D = x.shape
        N = B * S
        xt = x.reshape(N, D)
        logits = xt @ Wr + br
        probs = jax.nn.softmax(logits, axis=-1)
        top_p, top_idx = jax.lax.top_k(probs, TOP_K)
        weights = top_p / top_p.sum(axis=-1, keepdims=True)
        mu = xt.mean(axis=-1, keepdims=True)
        var = ((xt - mu) ** 2).mean(axis=-1, keepdims=True)
        xn = (xt - mu) * jax.lax.rsqrt(var + LN_EPS)
        xe = xn[None, :, :] * ln_g[:, None, :] + ln_b[:, None, :]
        h = jax.nn.gelu(jnp.einsum('end,edh->enh', xe, W1) + b1[:, None, :], approximate=False)
        y = jnp.einsum('enh,ehd->end', h, W2) + b2[:, None, :]
        y_tok = jnp.transpose(y, (1, 0, 2))
        sel = jnp.take_along_axis(y_tok, top_idx[:, :, None], axis=1)
        out = (weights[:, :, None] * sel).sum(axis=1)
        return out.reshape(B, S, D)
    x = x + _L0_gnn_ref(_layernorm(x, axis=-1), adj, L0_gnn_W_msg, L0_gnn_W_upd, L0_gnn_bias)
    x = x + _L0_ffn_ref(_layernorm(x, axis=-1), L0_ffn_Wr, L0_ffn_br, L0_ffn_ln_g, L0_ffn_ln_b, L0_ffn_W1, L0_ffn_b1, L0_ffn_W2, L0_ffn_b2)
    return x

_drawn_inputs = setup_inputs


def setup_inputs(seed=0):
    import zlib

    import numpy as np

    out = dict(_drawn_inputs(seed))
    spreads = {'L0_gnn_bias': (0.0, 0.1),
     'L0_ffn_br': (0.0, 0.1),
     'L0_ffn_ln_g': (1.0, 0.2),
     'L0_ffn_ln_b': (0.0, 0.1),
     'L0_ffn_b1': (0.0, 0.1),
     'L0_ffn_b2': (0.0, 0.1)}
    factors = {}
    for name, (base, spread) in spreads.items():
        noise = np.random.default_rng([zlib.crc32(name.encode()), seed]).standard_normal(out[name].shape)
        drawn = base * np.exp(spread * noise) if base else spread * noise
        out[name] = jnp.asarray(drawn.astype(out[name].dtype))
    for name, factor in factors.items():
        out[name] = (out[name] * factor).astype(out[name].dtype)
    return out
```

```python
import concourse.bass as bass
from concourse import mybir
from contextlib import ExitStack


def graph_then_experts_kernel(nc, x, adj, W_msg, W_upd, bias, Wr, br, ln_g, ln_b, W1, b1, W2, b2, out):
    fp32, fp16, i32, u32 = mybir.dt.float32, mybir.dt.float16, mybir.dt.int32, mybir.dt.uint32
    ALU = mybir.AluOpType
    ACT = mybir.ActivationFunctionType
    AX = mybir.AxisListType.X

    P = 128
    B, N, D = x.shape
    E, _, HID = W1.shape
    K = 2
    T = N // P
    C = HID // P
    NODES = B * N
    ROWS = 256
    SUB = ROWS // P
    REGION = NODES + ROWS
    TILES = K * NODES // ROWS + E - 1
    SPARE = E * REGION
    RW = D + 1
    NOWHERE = 1 << 20
    EPS = 1e-5
    WSCALE = 64.0
    FAR = 3e38

    rows = nc.dram_tensor("expert_rows", [SPARE + ROWS, RW], fp32, kind="Internal").ap()
    results = nc.dram_tensor("expert_results", [K * NODES, D], fp32, kind="Internal").ap()

    ctx = ExitStack()
    with ctx:
        def sb(name, shape, dt=fp32):
            return ctx.enter_context(nc.sbuf_tensor(name, shape, dt))

        def pb(name, shape, dt=fp32):
            return ctx.enter_context(nc.psum_tensor(name, shape, dt))

        def sem(name):
            return ctx.enter_context(nc.semaphore(name))

        ident = sb("ident", [P, P])
        earlier = sb("earlier", [P, P], fp16)
        ones16 = sb("ones16", [P, P], fp16)
        held = sb("held", [P, 1], fp16)
        ones_row = sb("ones_row", [1, P])
        expert_no = sb("expert_no", [P, T, E])
        expert_no8 = sb("expert_no8", [P, T, E])
        result_rows = sb("result_rows", [P, B, K, T], i32)
        br_all = sb("br_all", [P, E])
        bias_row = sb("bias_row", [1, D])
        b2_all = sb("b2_all", [P, E, D])
        pad_rows = sb("pad_rows", [P, SUB, RW])
        Wm_sb = sb("Wm_sb", [D, D])
        Wu_sb = sb("Wu_sb", [D, D])
        Wr_sb = sb("Wr_sb", [D, E])

        W1_sb = sb("W1_sb", [D, E, HID])
        W2_sb = sb("W2_sb", [P, E, C, D])
        W1h = sb("W1h", [D, E * HID], fp16)
        W1l = sb("W1l", [D, E * HID], fp16)
        W2h = sb("W2h", [P, E * C * D], fp16)
        W2l = sb("W2l", [P, E * C * D], fp16)
        gb_rows = sb("gb_rows", [2 * E, D])
        b1_rows = sb("b1_rows", [E * C, P])
        gain = sb("gain", [D, E])
        offset = sb("offset", [D, E])
        b1T = sb("b1T", [P, E * C])
        h_bias = sb("h_bias", [P, E * C])

        xin = [sb(f"xin{q}", [P, T, D]) for q in range(2)]
        adj_int = [sb(f"adj_int{q}", [P, T, N], i32) for q in range(2)]
        adj_f = [sb(f"adj_f{q}", [P, T, N]) for q in range(2)]
        xn = [sb(f"xn{q}", [P, T, D]) for q in range(2)]
        xnT = [sb(f"xnT{q}", [D, N]) for q in range(2)]
        msg = [sb(f"msg{q}", [P, T, D + 1]) for q in range(2)]
        upd = [sb(f"upd{q}", [P, T, D]) for q in range(2)]
        row = [sb(f"row{q}", [P, K, T, RW]) for q in range(2)]
        rowT = [sb(f"rowT{q}", [D, N]) for q in range(2)]
        member = [sb(f"member{q}", [P, T, E], fp16) for q in range(2)]
        dest = [sb(f"dest{q}", [P, K, T], u32) for q in range(2)]
        x2 = sb("x2", [P, B, T, D])
        summed = sb("summed", [P, T, D])
        statsA, statsB = sb("statsA", [P, T, 6]), sb("statsB", [P, T, 6])
        meanA, meanB = sb("meanA", [P, T]), sb("meanB", [P, T])
        spreadA, spreadB = sb("spreadA", [P, T]), sb("spreadB", [P, T])
        gapA, gapB = sb("gapA", [P, T]), sb("gapB", [P, T])
        gapA2, gapB2 = sb("gapA2", [P, T]), sb("gapB2", [P, T])
        veA = sb("veA", [P, T])
        sdA = sb("sdA", [P, T])
        rsA = sb("rsA", [P, T])
        veB = sb("veB", [P, T])
        sdB = sb("sdB", [P, T])
        rsB = sb("rsB", [P, T])
        vvB = sb("vvB", [P, T])
        ve2 = sb("ve2", [P, T])
        sd2 = [sb(f"sd2{q}", [P, T]) for q in range(2)]
        rs2 = sb("rs2", [P, T])
        rsBoth = sb("rsBoth", [P, T])
        degm = sb("degm", [P, T])
        degr = sb("degr", [P, T])
        degw = sb("degw", [P, T])
        lg0 = sb("lg0", [P, T, E])
        lg = sb("lg", [P, T, E])
        lg2 = sb("lg2", [P, T, E])
        top = sb("top", [P, K, T])
        hit = sb("hit", [P, T, E])
        key = sb("key", [P, T, E])
        chosen = sb("chosen", [P, T])
        onehot = sb("onehot", [P, K, T, E])
        pos = sb("pos", [P, T, E])
        picked = sb("picked", [P, K, T, E])
        free_row = sb("free_row", [P, E])
        margin = sb("margin", [P, B, T])

        free_int = sb("free_int", [1, E], i32)
        count = sb("count", [1, E])
        steps32 = sb("steps32", [1, E, NODES // ROWS])
        over = sb("over", [1, E, NODES // ROWS])
        ntile = sb("ntile", [1, E])
        upto = sb("upto", [1, E, E])
        prod = sb("prod", [1, E, E])
        tile_end = sb("tile_end", [1, E])
        jump = sb("jump", [1, E])
        tile_no = sb("tile_no", [1, TILES, E])
        past = sb("past", [1, TILES, E])
        moved = sb("moved", [1, TILES, E])
        t_expert = sb("t_expert", [1, TILES])
        t_row = sb("t_row", [1, TILES])
        tile_expert = sb("tile_expert", [1, TILES], i32)
        tile_row = sb("tile_row", [1, TILES], i32)

        tin = [sb(f"tin{q}", [P, SUB, RW]) for q in range(2)]
        result_row = sb("result_row", [P, TILES, SUB], u32)
        tTh = [sb(f"tTh{q}", [D, ROWS], fp16) for q in range(2)]
        tTl = [sb(f"tTl{q}", [D, ROWS], fp16) for q in range(2)]
        gel = [adj_f[q][:, 0:T // 2, :].rearrange("p a (c r) -> p (a c) r", r=ROWS) for q in range(2)]
        halves = [adj_int[q][:, :, :].bitcast(fp16).rearrange("p a (c r) -> p (a c) r", r=ROWS) for q in range(2)]
        gelh = [halves[q][:, 0:C, :] for q in range(2)]
        gell = [halves[q][:, C:2 * C, :] for q in range(2)]
        y = [sb(f"y{q}", [P, SUB, D]) for q in range(2)]
        send_to = [sb(f"send_to{q}", [P, SUB], u32) for q in range(2)]

        weight = sb("weight", [P, K, B * T])
        ex = sb("ex", [P, B * T])
        ex1 = sb("ex1", [P, B * T])
        yk = [adj_f[q][:, T // 2:T, :].rearrange("p k (t d) -> p k t d", t=T) for q in range(2)]
        second = [sb(f"second{q}", [P, T, D]) for q in range(2)]
        first = sb("first", [P, T, D])
        total = [sb(f"total{q}", [P, T, D]) for q in range(2)]

        bank = [pb(f"bank{i}", [P, 512]) for i in range(3)]
        ps_xnT, ps_msg, ps_upd = bank
        ps_sum = pb("ps_sum", [P, T, 256])
        ps_rowT = pb("ps_rowT", [P, 512])
        ps_logit = pb("ps_logit", [P, 512])
        ps_rank = pb("ps_rank", [P, 512])
        ps_h = [[ps_xnT, ps_msg], [ps_sum[:, 0:2, :].rearrange("p a b -> p (a b)"), ps_sum[:, 2:4, :].rearrange("p a b -> p (a b)")]]
        ps_tT = [ps_upd, ps_rowT]
        ps_y = [ps_logit, ps_rank]

        names = """x_in0 x_in1 adj_in0 adj_in1 const_in w_in
            const_id0 const_id const_tri0 const_tri const_pool const_dve
            bnA gapA aggA veA sdA rsA xn xnT_ps xnT msg_ps upd_ps msg upd adj_f
            sum_ps degm degr degw summed x2 bnB gapB aggB veB sdB rsB vvB ve20 ve2 sd2 rs2 rsBoth ids row
            rowT_ps rowT row_copied logit_ps lg0 lg top1 hit1 key1 chosen1 onehot1 lg2 top2 hit2 key2 chosen2 onehot2
            member margin rank_ps pos picked dest free_row scattered0 scattered1
            gbT_ps gain offset b1_ps b1T hb_ps h_bias w1h w1l w2h w2l
            cnt over ntile prod tile_end jump past texp t_expert moved t_row0 t_row1 table free_int
            pads held
            tin0 tin1 tT_ps tTh tTl result_row h_ps gel gelh gell y_ps y sent0 sent1
            ex ex1 wt0 weight yk0 yk1 second first total stored0 stored1""".split()
        s = {n: sem(n) for n in names}

        const_loads = [(Wm_sb[:, :], W_msg), (Wu_sb[:, :], W_upd),
                       (bias_row[:, :], bias.rearrange("(a n) -> a n", a=1)), (Wr_sb[:, :], Wr),
                       (br_all[:, :], br.rearrange("(a n) -> a n", a=1).broadcast_to([P, E]))]
        weight_loads = [(gb_rows[0:E, :], ln_g), (gb_rows[E:2 * E, :], ln_b),
                        (b1_rows[:, :], b1.rearrange("e (c p) -> (e c) p", p=P)),
                        (W1_sb[:, :, :], W1.rearrange("e d h -> d e h")),
                        (W2_sb[:, :, :, :], W2.rearrange("e (c h) d -> h e c d", h=P)),
                        (b2_all[:, :, :], b2.rearrange("(a e) d -> a e d", a=1).broadcast_to([P, E, D]))]

        block = ctx.enter_context(nc.Block())

        def graph_steps(eng, step):
            for n in range(4):
                step(n, n % 2)
            with eng.Fori(4, B - 3, 2) as n:
                step(n, 0)
                step(n + 1, 1)
            for n in (B - 2, B - 1, B, B + 1):
                step(n, n % 2)

        def tile_steps(eng, step):
            for n in range(4):
                step(n, n % 2)
            with eng.Fori(4, TILES - 2, 2) as n:
                step(n, 0)
                step(n + 1, 1)
            for n in (TILES - 1, TILES, TILES + 1):
                step(n, n % 2)

        def has(n, lag, count=B):
            return not isinstance(n, int) or 0 <= n - lag < count

        def later(n, least):
            return not isinstance(n, int) or n >= least

        def loaded(eng, name, n, q, each=16):
            eng.wait_ge(s[f"{name}{q}"], each * (n // 2 + 1) if isinstance(n, int) else (n - q) * (each // 2) + each)

        def at(n):
            return slice(n, n + 1) if isinstance(n, int) else bass.ds(n, 1)

        def graph(tensor, b):
            return tensor[at(b)]

        @block.sync
        def _(sp):
            def load(b, q):
                if later(b, 2):
                    sp.wait_ge(s["x2"], b - 1)
                sp.dma_start(xin[q][:, :, :], graph(x, b).rearrange("o (t p) d -> p (o t) d", p=P)).then_inc(s[f"x_in{q}"], 16)
                if later(b, 2):
                    sp.wait_ge(s["adj_f"], b - 1)
                sp.dma_start(adj_int[q][:, :, :], graph(adj, b).rearrange("o (t p) n -> p (o t) n", p=P)).then_inc(s[f"adj_in{q}"], 16)

            load(0, 0)
            for dst, src in const_loads:
                sp.dma_start(dst, src).then_inc(s["const_in"], 16)
            load(1, 1)
            for dst, src in weight_loads:
                sp.dma_start(dst, src).then_inc(s["w_in"], 16)
            with sp.Fori(2, B - 1, 2) as b:
                load(b, 0)
                load(b + 1, 1)

            sp.wait_ge(s["const_pool"], 1)
            sp.wait_ge(s["free_int"], 1)
            for e in range(E):
                start = sp.value_load(free_int[0:1, e:e + 1], min_val=e * REGION, max_val=e * REGION + NODES)
                sp.dma_start(rows[bass.ds(start, ROWS), :].rearrange("(s p) w -> p s w", p=P), pad_rows[:, :, :]).then_inc(s["pads"], 16)
            sp.dma_start(rows[SPARE:SPARE + ROWS, :].rearrange("(s p) w -> p s w", p=P), pad_rows[:, :, :]).then_inc(s["pads"], 16)

            sp.wait_ge(s["pads"], 16 * (E + 1))
            for q in range(2):
                sp.wait_ge(s[f"scattered{q}"], 16 * K * T * (B // 2))
            sp.wait_ge(s["table"], 1)

            def load_tile(t, q):
                start = sp.value_load(tile_row[0:1, at(t)], min_val=0, max_val=SPARE)
                if later(t, 2):
                    sp.wait_ge(s["tT_ps"], t - 1)
                    sp.wait_ge(s["result_row"], t - 1)
                sp.dma_start(tin[q][:, :, :], rows[bass.ds(start, ROWS), :].rearrange("(s p) w -> p s w", p=P)).then_inc(s[f"tin{q}"], 16)

            load_tile(0, 0)
            load_tile(1, 1)
            with sp.Fori(2, TILES - 2, 2) as t:
                load_tile(t, 0)
                load_tile(t + 1, 1)
            load_tile(TILES - 1, 0)

            for q in range(2):
                sp.wait_ge(s[f"sent{q}"], 16 * SUB * ((TILES + 1 - q) // 2))
            by_graph = results.rearrange("(k b t p) d -> b k p t d", k=K, b=B, p=P)

            def load_results(b, q):
                if later(b, 2):
                    sp.wait_ge(s["first"], b - 1)
                    sp.wait_ge(s["second"], b - 1)
                for k in range(K):
                    sp.dma_start(yk[q][:, k, :, :], graph(by_graph, b)[:, k].rearrange("o p t d -> p (o t) d")).then_inc(s[f"yk{q}"], 16)

            load_results(0, 0)
            load_results(1, 1)
            with sp.Fori(2, B - 1, 2) as b:
                load_results(b, 0)
                load_results(b + 1, 1)

        @block.gpsimd
        def _(pool):
            pool.memset(ident[:, :], 0.0).then_inc(s["const_id0"], 1)
            pool.wait_ge(s["const_id0"], 1)
            pool.affine_select(out=ident[:, :], in_=ident[:, :], compare_op=ALU.not_equal, fill=1.0,
                               base=0, pattern=[[-1, P]], channel_multiplier=1).then_inc(s["const_id"], 1)
            pool.memset(earlier[:, :], 0.0).then_inc(s["const_tri0"], 1)
            pool.wait_ge(s["const_tri0"], 1)
            pool.affine_select(out=earlier[:, :], in_=earlier[:, :], compare_op=ALU.is_ge, fill=1.0,
                               base=0, pattern=[[-1, P]], channel_multiplier=1).then_inc(s["const_tri"], 1)
            pool.memset(ones16[:, :], 1.0)
            pool.memset(upto[:, :, :], 0.0).then_inc(s["const_tri0"], 1)
            pool.wait_ge(s["const_tri0"], 2)
            pool.affine_select(out=upto[:, :, :], in_=upto[:, :, :], compare_op=ALU.is_gt, fill=1.0,
                               base=0, pattern=[[-1, E], [1, E]], channel_multiplier=0)
            pool.iota(expert_no[:, :, :], pattern=[[0, T], [1, E]], base=0, channel_multiplier=0,
                      allow_small_or_imprecise_dtypes=True)
            pool.iota(expert_no8[:, :, :], pattern=[[0, T], [1, E]], base=E, channel_multiplier=0,
                      allow_small_or_imprecise_dtypes=True)
            pool.iota(result_rows[:, :, :, :], pattern=[[N, B], [NODES, K], [P, T]], base=0, channel_multiplier=1)
            pool.iota(free_row[:, :], pattern=[[REGION, E]], base=0, channel_multiplier=0,
                      allow_small_or_imprecise_dtypes=True)
            pool.iota(steps32[:, :, :], pattern=[[0, E], [ROWS, NODES // ROWS]], base=0, channel_multiplier=0,
                      allow_small_or_imprecise_dtypes=True)
            pool.iota(tile_no[:, :, :], pattern=[[1, TILES], [0, E]], base=0, channel_multiplier=0,
                      allow_small_or_imprecise_dtypes=True)
            pool.memset(pad_rows[:, :, 0:D], 0.0)
            pool.memset(pad_rows[:, :, D:RW].bitcast(i32), NOWHERE)
            pool.memset(ones_row[:, :], 1.0).then_inc(s["const_pool"], 1)

            def hold(before):
                if later(before, 1):
                    pool.wait_ge(s["held"], before)
                pool.tensor_tensor(held[:, :], ones16[:, 0:1], ones16[:, 0:1], ALU.mult).then_inc(s["held"], 1)

            def scatter(n, q):
                if not has(n, 2):
                    return
                b = n - 2
                pool.wait_ge(s["dest"], b + 1)
                pool.wait_ge(s["row_copied"], b + 1)
                hold(b)
                for k in range(K):
                    for t in range(T):
                        pool.indirect_dma_start(rows, bass.IndirectOffsetOnAxis(ap=dest[q][:, k, t:t + 1], axis=0),
                                                row[q][:, k, t, :], None).then_inc(s[f"scattered{q}"], 16)

            graph_steps(pool, scatter)

            def send(t, q):
                pool.wait_ge(s["y"], t + 1)
                hold(t + B)
                for u in range(SUB):
                    idx = send_to[q][:, u:u + 1]
                    pool.indirect_dma_start(results, bass.IndirectOffsetOnAxis(ap=idx, axis=0), y[q][:, u, :], None,
                                            bounds_check=K * NODES - 1, oob_is_err=False).then_inc(s[f"sent{q}"], 16)

            with pool.Fori(0, TILES - 2, 2) as t:
                send(t, 0)
                send(t + 1, 1)
            send(TILES - 1, 0)

        @block.tensor
        def _(pe):
            pe.wait_ge(s["const_id"], 1)
            pe.wait_ge(s["const_tri"], 1)
            pe.wait_ge(s["const_pool"], 1)
            pe.wait_ge(s["const_in"], 16 * len(const_loads))

            def route(n, q):
                b = n - 2
                pe.wait_ge(s["row"], b + 1)
                if later(b, 1):
                    pe.wait_ge(s["rowT"], b)
                for t in range(T):
                    last = pe.transpose(ps_rowT[:, t * P:(t + 1) * P], row[q][:, 0, t, 0:D], ident[:, :])
                last.then_inc(s["rowT_ps"], 1)
                pe.wait_ge(s["rowT"], b + 1)
                if later(b, 1):
                    pe.wait_ge(s["lg0"], b)
                for t in range(T):
                    last = pe.matmul(ps_logit[:, t * E:(t + 1) * E], rowT[q][:, t * P:(t + 1) * P], Wr_sb[:, :],
                                     start=True, stop=True)
                last.then_inc(s["logit_ps"], 1)

            def neighbours(n, q):
                b = n - 1
                pe.wait_ge(s["msg"], b + 1)
                pe.wait_ge(s["adj_f"], b + 1)
                if later(b, 1):
                    pe.wait_ge(s["summed"], b)
                for j in range(T):
                    for i in range(T):
                        last = pe.matmul(ps_sum[:, j, 0:D + 1], adj_f[q][:, i, j * P:(j + 1) * P], msg[q][:, i, :],
                                         start=(i == 0), stop=(i == T - 1))
                last.then_inc(s["sum_ps"], 1)

            def rank(n, q):
                b = n - 2
                pe.wait_ge(s["member"], b + 1)
                if later(b, 1):
                    pe.wait_ge(s["free_row"], b)
                m = member[q]
                pe.matmul(ps_rank[:, 0:T * E], earlier[:, :], m[:, :, :].rearrange("p t e -> p (t e)"), start=True, stop=False)
                for k in range(1, T):
                    pe.matmul(ps_rank[:, k * E:T * E], ones16[:, :], m[:, 0:T - k, :].rearrange("p t e -> p (t e)"),
                              start=False, stop=(k == T - 1))
                for t in range(T):
                    last = pe.matmul(ps_rank[:, T * E:(T + 1) * E], ones16[:, :], m[:, t, :], start=(t == 0), stop=(t == T - 1))
                last.then_inc(s["rank_ps"], 1)

            def products(n, q):
                b = n
                pe.wait_ge(s["xn"], b + 1)
                if later(b, 1):
                    pe.wait_ge(s["xnT"], b)
                for t in range(T):
                    last = pe.transpose(ps_xnT[:, t * P:(t + 1) * P], xn[q][:, t, :], ident[:, :])
                last.then_inc(s["xnT_ps"], 1)
                pe.wait_ge(s["xnT"], b + 1)
                if later(b, 1):
                    pe.wait_ge(s["msg"], b)
                for t in range(T):
                    last = pe.matmul(ps_msg[:, t * D:(t + 1) * D], xnT[q][:, t * P:(t + 1) * P], Wm_sb[:, :],
                                     start=True, stop=True)
                last.then_inc(s["msg_ps"], 1)
                if later(b, 1):
                    pe.wait_ge(s["upd"], b)
                for t in range(T):
                    pe.matmul(ps_upd[:, t * D:(t + 1) * D], xnT[q][:, t * P:(t + 1) * P], Wu_sb[:, :],
                              start=True, stop=False)
                    last = pe.matmul(ps_upd[:, t * D:(t + 1) * D], ones_row[:, :], bias_row[:, :],
                                     start=False, stop=True)
                last.then_inc(s["upd_ps"], 1)

            def step(n, q):
                if has(n, 2):
                    route(n, q)
                if has(n, 1):
                    neighbours(n, 1 - q)
                if has(n, 2):
                    rank(n, q)
                if has(n, 0):
                    products(n, q)

            graph_steps(pe, step)

            pe.wait_ge(s["w_in"], 16 * len(weight_loads))
            pe.transpose(ps_rowT[:, 0:2 * E], gb_rows[:, :], ident[0:2 * E, 0:2 * E])
            pe.transpose(ps_rowT[:, 2 * E:2 * E + E * C], b1_rows[:, :], ident[0:E * C, 0:E * C]).then_inc(s["gbT_ps"], 1)
            pe.wait_ge(s["offset"], 1)
            pe.wait_ge(s["upd"], B)
            for e in range(E):
                for c in range(C):
                    last = pe.matmul(ps_upd[:, e * C + c:e * C + c + 1], W1_sb[:, e, c * P:(c + 1) * P], offset[:, e:e + 1],
                                     start=True, stop=True)
            last.then_inc(s["hb_ps"], 1)

            pe.wait_ge(s["table"], 1)
            pe.wait_ge(s["h_bias"], 1)
            pe.wait_ge(s["w1l"], 1)
            pe.wait_ge(s["w2l"], 1)

            def expert(t):
                return pe.value_load(tile_expert[0:1, at(t)], min_val=0, max_val=E - 1)

            def turn(t, q):
                loaded(pe, "tin", t, q)
                if later(t, 2):
                    pe.wait_ge(s["tTl"], t - 1)
                for u in range(SUB):
                    last = pe.transpose(ps_tT[q][:, u * P:(u + 1) * P], tin[q][:, u, 0:D], ident[:, :])
                last.then_inc(s["tT_ps"], 1)

            def hidden(t, q, e):
                pe.wait_ge(s["tTl"], t + 1)
                pe.wait_ge(s["tTh"], t + 1)
                for half in range(2):
                    if later(t, 2):
                        pe.wait_ge(s["gel"], 2 * (t - 2) + half + 1)
                    for c2 in range(C // 2):
                        c = half * (C // 2) + c2
                        w = slice_of(e, HID, c * P)
                        to = ps_h[q][half][:, c2 * ROWS:(c2 + 1) * ROWS]
                        pe.matmul(to, W1h[:, w], tTh[q][:, :], start=True, stop=False)
                        pe.matmul(to, W1h[:, w], tTl[q][:, :], start=False, stop=False)
                        last = pe.matmul(to, W1l[:, w], tTh[q][:, :], start=False, stop=True)
                    last.then_inc(s["h_ps"], 1)

            def slice_of(e, width, at):
                return bass.ds(e * width + at, P)

            def output(t, q, e):
                if later(t, 2):
                    pe.wait_ge(s["y"], t - 1)
                for u in range(SUB):
                    to = ps_y[q][:, u * D:(u + 1) * D]
                    for c in range(C):
                        if u == 0 and c % (C // 2) == 0:
                            pe.wait_ge(s["gell"], 2 * t + c // (C // 2) + 1)
                        w = slice_of(e, C * D, c * D)
                        gh = gelh[q][:, c, u * P:(u + 1) * P]
                        gl = gell[q][:, c, u * P:(u + 1) * P]
                        pe.matmul(to, gh, W2h[:, w], start=(c == 0), stop=False)
                        pe.matmul(to, gh, W2l[:, w], start=False, stop=False)
                        last = pe.matmul(to, gl, W2h[:, w], start=False, stop=(c == C - 1))
                last.then_inc(s["y_ps"], 1)

            def tile_step(n, q):
                if has(n, -1, TILES):
                    turn(n + 1, 1 - q)
                if has(n, 0, TILES):
                    hidden(n, q, expert(n))
                if has(n, 1, TILES):
                    output(n - 1, 1 - q, expert(n - 1))

            turn(0, 0)
            tile_steps(pe, tile_step)

        @block.scalar
        def _(act):
            def step(n, q):
                if has(n, 2):
                    b = n - 2
                    act.wait_ge(s["rowT_ps"], b + 1)
                    act.activation(rowT[q][:, :], ps_rowT[:, :], ACT.Copy).then_inc(s["rowT"], 1)
                if has(n, 0):
                    b = n
                    loaded(act, "adj_in", b, q)
                    if later(b, 2):
                        act.wait_ge(s["sum_ps"], b - 1)
                    act.activation(adj_f[q][:, :, :], adj_int[q][:, :, :], ACT.Copy).then_inc(s["adj_f"], 1)
                if has(n, 2):
                    b = n - 2
                    act.wait_ge(s["row"], b + 1)
                    act.activation(row[q][:, 1, :, 0:D], row[q][:, 0, :, 0:D], ACT.Copy).then_inc(s["row_copied"], 1)
                if has(n, 0):
                    b = n
                    act.wait_ge(s["xnT_ps"], b + 1)
                    if later(b, 2):
                        act.wait_ge(s["upd_ps"], b - 1)
                    act.activation(xnT[q][:, :], ps_xnT[:, :], ACT.Copy).then_inc(s["xnT"], 1)
                if has(n, 1):
                    b = n - 1
                    act.wait_ge(s["veB"], b + 1)
                    if later(b, 1):
                        act.wait_ge(s["rsB"], b)
                    act.activation(sdB[:, :], veB[:, :], ACT.Sqrt).then_inc(s["sdB"], 1)
                if has(n, 0):
                    b = n
                    act.wait_ge(s["msg_ps"], b + 1)
                    if later(b, 2):
                        act.wait_ge(s["sum_ps"], b - 1)
                    act.activation(msg[q][:, :, 0:D], ps_msg[:, :].rearrange("p (t d) -> p t d", t=T), ACT.Copy).then_inc(s["msg"], 1)
                if has(n, 1):
                    b = n - 1
                    act.wait_ge(s["ve2"], b + 1)
                    act.activation(sd2[1 - q][:, :], ve2[:, :], ACT.Sqrt).then_inc(s["sd2"], 1)
                if has(n, 0):
                    b = n
                    act.wait_ge(s["upd_ps"], b + 1)
                    if later(b, 2):
                        act.wait_ge(s["summed"], b - 1)
                    act.activation(upd[q][:, :, :], ps_upd[:, :].rearrange("p (t d) -> p t d", t=T), ACT.Copy).then_inc(s["upd"], 1)
                if has(n, -1):
                    b = n + 1
                    act.wait_ge(s["veA"], b + 1)
                    if later(b, 1):
                        act.wait_ge(s["rsA"], b)
                    act.activation(sdA[:, :], veA[:, :], ACT.Sqrt).then_inc(s["sdA"], 1)

            act.wait_ge(s["const_dve"], 1)
            act.wait_ge(s["veA"], 1)
            act.activation(sdA[:, :], veA[:, :], ACT.Sqrt).then_inc(s["sdA"], 1)
            graph_steps(act, step)

            act.wait_ge(s["gbT_ps"], 1)
            act.mul(gain[:, :], ps_rowT[:, 0:E], WSCALE).then_inc(s["gain"], 1)
            act.activation(offset[:, :], ps_rowT[:, E:2 * E], ACT.Copy).then_inc(s["offset"], 1)
            act.activation(b1T[:, :], ps_rowT[:, 2 * E:2 * E + E * C], ACT.Copy).then_inc(s["b1T"], 1)
            act.wait_ge(s["gain"], 1)
            act.wait_ge(s["w_in"], 16 * len(weight_loads))
            for e in range(E):
                last = act.activation(W1h[:, e * HID:(e + 1) * HID], W1_sb[:, e, :], ACT.Copy, scale=gain[:, e:e + 1])
            last.then_inc(s["w1h"], 1)
            act.mul(W2h[:, :], W2_sb[:, :, :, :].rearrange("p e c d -> p (e c d)"), WSCALE).then_inc(s["w2h"], 1)
            act.wait_ge(s["margin"], B)
            act.activation(ex[:, :], margin[:, :, :].rearrange("p b t -> p (b t)"), ACT.Exp).then_inc(s["ex"], 1)

            act.wait_ge(s["h_bias"], 1)
            act.wait_ge(s["table"], 1)

            def high(t, q):
                act.wait_ge(s["tT_ps"], t + 1)
                if later(t, 2):
                    act.wait_ge(s["h_ps"], 2 * (t - 1))
                act.activation(tTh[q][:, :], ps_tT[q][:, 0:ROWS], ACT.Copy).then_inc(s["tTh"], 1)

            def gelu(t, q):
                e = act.value_load(tile_expert[0:1, at(t)], min_val=0, max_val=E - 1)
                for half in range(2):
                    act.wait_ge(s["h_ps"], 2 * t + half + 1)
                    if later(t, 2):
                        act.wait_ge(s["gell"], 2 * (t - 2) + half + 1)
                    for c2 in range(C // 2):
                        c = half * (C // 2) + c2
                        last = act.activation(gel[q][:, c, :], ps_h[q][half][:, c2 * ROWS:(c2 + 1) * ROWS], ACT.Gelu,
                                              bias=h_bias[:, bass.ds(e * C + c, 1)], scale=1.0 / WSCALE)
                    last.then_inc(s["gel"], 1)

            def tile_step(n, q):
                if has(n, -1, TILES):
                    high(n + 1, 1 - q)
                if has(n, 0, TILES):
                    gelu(n, q)

            high(0, 0)
            tile_steps(act, tile_step)

            act.wait_ge(s["weight"], 1)

            def weighted_second(b, q):
                loaded(act, "yk", b, q, 16 * K)
                if later(b, 2):
                    act.wait_ge(s["total"], b - 1)
                for t in range(T):
                    last = act.activation(second[q][:, t, :], yk[q][:, 1, t, :], ACT.Copy, scale=weight[:, 1, at(b * T + t)])
                last.then_inc(s["second"], 1)

            def store(b, q):
                act.wait_ge(s["total"], b + 1)
                act.dma_start(graph(out, b).rearrange("o (t p) d -> p (o t) d", p=P), total[q][:, :, :]).then_inc(s[f"stored{q}"], 16)

            def pair(b):
                weighted_second(b + 1, 1)
                store(b, 0)
                weighted_second(b + 2, 0)
                store(b + 1, 1)

            weighted_second(0, 0)
            pair(0)
            with act.Fori(2, B - 3, 2) as b:
                pair(b)
            weighted_second(B - 1, 1)
            store(B - 2, 0)
            store(B - 1, 1)
            for q in range(2):
                act.wait_ge(s[f"stored{q}"], 16 * (B // 2))

        @block.vector
        def _(dve):
            for q in range(2):
                last = dve.memset(msg[q][:, :, D:D + 1], 1.0)
            last.then_inc(s["const_dve"], 1)
            dve.wait_ge(s["const_pool"], 1)
            dve.wait_ge(s["const_in"], 16 * len(const_loads))

            def wide(a, n=E):
                return a.unsqueeze(2).to_broadcast([P, T, n])

            def aggregate(b, stats, mean, spread, gap, gap2, ve, which):
                dve.tensor_tensor(spread[:, :], stats[:, :, 2], stats[:, :, 5], ALU.add)
                dve.tensor_tensor(gap[:, :], stats[:, :, 1], stats[:, :, 4], ALU.subtract)
                dve.tensor_tensor(mean[:, :], stats[:, :, 1], stats[:, :, 4], ALU.add).then_inc(s[f"gap{which}"], 1)
                dve.wait_ge(s[f"gap{which}"], b + 1)
                dve.tensor_tensor(gap2[:, :], gap[:, :], gap[:, :], ALU.mult)
                dve.tensor_scalar(mean[:, :], mean[:, :], 0.5, None, ALU.mult)
                dve.tensor_scalar(spread[:, :], spread[:, :], 1.0 / D, EPS, ALU.mult, ALU.add).then_inc(s[f"agg{which}"], 1)
                dve.wait_ge(s[f"agg{which}"], b + 1)
                dve.scalar_tensor_tensor(ve[:, :], gap2[:, :], 0.25, spread[:, :], ALU.mult, ALU.add).then_inc(s[f"ve{which}"], 1)

            def moments(b, q):
                loaded(dve, "x_in", b, q)
                if later(b, 1):
                    dve.wait_ge(s["xn"], b)
                for t in range(T):
                    last = dve.bn_stats(statsA[:, t, :], xin[q][:, t, :])
                last.then_inc(s["bnA"], 1)
                dve.wait_ge(s["bnA"], b + 1)
                aggregate(b, statsA, meanA, spreadA, gapA, gapA2, veA, "A")

            def normalise(b, q):
                dve.wait_ge(s["sdA"], b + 1)
                dve.reciprocal(rsA[:, :], sdA[:, :]).then_inc(s["rsA"], 1)
                dve.wait_ge(s["rsA"], b + 1)
                if later(b, 2):
                    dve.wait_ge(s["xnT_ps"], b - 1)
                for t in range(T):
                    last = dve.tensor_scalar(xn[q][:, t, :], xin[q][:, t, :], meanA[:, t:t + 1], rsA[:, t:t + 1],
                                             ALU.subtract, ALU.mult)
                last.then_inc(s["xn"], 1)

            def residual(b, q):
                deg = ps_sum[:, :, D:D + 1].rearrange("p t a -> p (t a)")
                dve.wait_ge(s["sum_ps"], b + 1)
                dve.tensor_scalar(degm[:, :], deg, 1.0, None, ALU.max).then_inc(s["degm"], 1)
                dve.wait_ge(s["degm"], b + 1)
                dve.reciprocal(degr[:, :], degm[:, :]).then_inc(s["degr"], 1)
                dve.wait_ge(s["degr"], b + 1)
                dve.scalar_tensor_tensor(degw[:, :], deg, 0.0, degr[:, :], ALU.is_gt, ALU.mult).then_inc(s["degw"], 1)
                dve.wait_ge(s["degw"], b + 1)
                dve.wait_ge(s["upd"], b + 1)
                for t in range(T):
                    last = dve.scalar_tensor_tensor(summed[:, t, :], ps_sum[:, t, 0:D], degw[:, t:t + 1], upd[q][:, t, :],
                                                    ALU.mult, ALU.add)
                last.then_inc(s["summed"], 1)
                dve.wait_ge(s["summed"], b + 1)
                dve.scalar_tensor_tensor(graph_x2(b), summed[:, :, :], 0.0, xin[q][:, :, :], ALU.max, ALU.add)\
                   .then_inc(s["x2"], 1)
                dve.wait_ge(s["const_dve"], 1)
                dve.wait_ge(s["x2"], b + 1)
                for t in range(T):
                    last = dve.bn_stats(statsB[:, t, :], block_x2(b, t))
                last.then_inc(s["bnB"], 1)
                dve.wait_ge(s["bnB"], b + 1)
                aggregate(b, statsB, meanB, spreadB, gapB, gapB2, veB, "B")

            def graph_x2(b):
                return x2[:, at(b), :, :].rearrange("p o t d -> p (o t) d")

            def block_x2(b, t):
                return x2[:, at(b), t, :].rearrange("p o d -> p (o d)")

            def inner_variance(b):
                dve.wait_ge(s["sdB"], b + 1)
                dve.reciprocal(rsB[:, :], sdB[:, :]).then_inc(s["rsB"], 1)
                dve.wait_ge(s["rsB"], b + 1)
                dve.scalar_tensor_tensor(vvB[:, :], veB[:, :], EPS, rsB[:, :], ALU.subtract, ALU.mult).then_inc(s["vvB"], 1)
                dve.wait_ge(s["vvB"], b + 1)
                dve.tensor_tensor(ve2[:, :], vvB[:, :], rsB[:, :], ALU.mult).then_inc(s["ve20"], 1)
                dve.wait_ge(s["ve20"], b + 1)
                dve.tensor_scalar(ve2[:, :], ve2[:, :], EPS, None, ALU.add).then_inc(s["ve2"], 1)

            def make_rows(b, q):
                dve.wait_ge(s["sd2"], b + 1)
                dve.reciprocal(rs2[:, :], sd2[q][:, :]).then_inc(s["rs2"], 1)
                dve.wait_ge(s["rs2"], b + 1)
                dve.tensor_tensor(rsBoth[:, :], rsB[:, :], rs2[:, :], ALU.mult).then_inc(s["rsBoth"], 1)
                dve.wait_ge(s["rsBoth"], b + 1)
                if later(b, 2):
                    dve.wait_ge(s[f"scattered{q}"], 16 * K * T * (b // 2) if isinstance(b, int) else 8 * K * T * (b - q))
                dve.tensor_copy(row[q][:, :, :, D:RW].bitcast(i32).rearrange("p k t a -> p k (t a)"),
                                result_rows[:, at(b), :, :].rearrange("p o k t -> p (o k) t"))
                for t in range(T):
                    last = dve.tensor_scalar(row[q][:, 0, t, 0:D], block_x2(b, t), meanB[:, t:t + 1], rsBoth[:, t:t + 1],
                                             ALU.subtract, ALU.mult)
                last.then_inc(s["row"], 1)

            def choose(b, k, logits):
                dve.tensor_reduce(top[:, k, :], logits, AX, ALU.max).then_inc(s[f"top{k + 1}"], 1)
                dve.wait_ge(s[f"top{k + 1}"], b + 1)
                dve.tensor_tensor(hit[:, :, :], logits, wide(top[:, k, :]), ALU.is_equal).then_inc(s[f"hit{k + 1}"], 1)
                dve.wait_ge(s[f"hit{k + 1}"], b + 1)
                dve.scalar_tensor_tensor(key[:, :, :], hit[:, :, :], -float(E), expert_no8[:, :, :], ALU.mult, ALU.add)\
                   .then_inc(s[f"key{k + 1}"], 1)
                dve.wait_ge(s[f"key{k + 1}"], b + 1)
                dve.tensor_reduce(chosen[:, :], key[:, :, :], AX, ALU.min).then_inc(s[f"chosen{k + 1}"], 1)
                dve.wait_ge(s[f"chosen{k + 1}"], b + 1)
                dve.tensor_tensor(onehot[:, k, :, :], expert_no[:, :, :], wide(chosen[:, :]), ALU.is_equal)\
                   .then_inc(s[f"onehot{k + 1}"], 1)
                dve.wait_ge(s[f"onehot{k + 1}"], b + 1)

            def route(b, q):
                dve.wait_ge(s["logit_ps"], b + 1)
                dve.tensor_tensor(lg0[:, :, :], ps_logit[:, 0:T * E].rearrange("p (t e) -> p t e", t=T), wide(sd2[q][:, :]), ALU.mult)\
                   .then_inc(s["lg0"], 1)
                dve.wait_ge(s["lg0"], b + 1)
                dve.tensor_tensor(lg[:, :, :], lg0[:, :, :], br_all[:, :].unsqueeze(1).to_broadcast([P, T, E]), ALU.add)\
                   .then_inc(s["lg"], 1)
                dve.wait_ge(s["lg"], b + 1)
                choose(b, 0, lg[:, :, :])
                dve.scalar_tensor_tensor(lg2[:, :, :], onehot[:, 0, :, :], -FAR, lg[:, :, :], ALU.mult, ALU.add)\
                   .then_inc(s["lg2"], 1)
                dve.wait_ge(s["lg2"], b + 1)
                choose(b, 1, lg2[:, :, :])
                dve.tensor_tensor(member[q][:, :, :], onehot[:, 0, :, :], onehot[:, 1, :, :], ALU.add).then_inc(s["member"], 1)
                dve.tensor_tensor(margin[:, at(b), :].rearrange("p o t -> p (o t)"), top[:, 1, :], top[:, 0, :], ALU.subtract)\
                   .then_inc(s["margin"], 1)

            def place(b, q):
                dve.wait_ge(s["rank_ps"], b + 1)
                if later(b, 1):
                    dve.wait_ge(s["free_row"], b)
                dve.tensor_tensor(pos[:, :, :], ps_rank[:, 0:T * E].rearrange("p (t e) -> p t e", t=T),
                                  free_row[:, :].unsqueeze(1).to_broadcast([P, T, E]), ALU.add).then_inc(s["pos"], 1)
                dve.wait_ge(s["pos"], b + 1)
                dve.tensor_tensor(picked[:, :, :, :], onehot[:, :, :, :], pos[:, :, :].unsqueeze(1).to_broadcast([P, K, T, E]), ALU.mult)\
                   .then_inc(s["picked"], 1)
                dve.tensor_tensor(free_row[:, :], free_row[:, :], ps_rank[:, T * E:(T + 1) * E], ALU.add).then_inc(s["free_row"], 1)
                dve.wait_ge(s["picked"], b + 1)
                with nc.allow_low_precision(reason="summed in float32: one whole number under 2 ** 24, and zeros"):
                    dve.tensor_reduce(dest[q][:, :, :], picked[:, :, :, :], AX, ALU.add).then_inc(s["dest"], 1)

            def step(n, q):
                if has(n, 2):
                    route(n - 2, q)
                if has(n, 0):
                    normalise(n, q)
                if has(n, 1):
                    residual(n - 1, 1 - q)
                if has(n, 2):
                    place(n - 2, q)
                if has(n, 1):
                    inner_variance(n - 1)
                if has(n, -1):
                    moments(n + 1, 1 - q)
                if has(n, 1):
                    make_rows(n - 1, 1 - q)

            moments(0, 0)
            graph_steps(dve, step)

            dve.wait_ge(s["free_row"], B)
            dve.tensor_copy(free_int[:, :], free_row[0:1, :]).then_inc(s["free_int"], 1)
            dve.scalar_tensor_tensor(count[:, :], expert_no[0:1, 0, :], -float(REGION), free_row[0:1, :], ALU.mult, ALU.add)\
               .then_inc(s["cnt"], 1)
            dve.wait_ge(s["cnt"], 1)
            dve.tensor_tensor(over[:, :, :], count[:, :].unsqueeze(2).to_broadcast([1, E, NODES // ROWS]), steps32[:, :, :], ALU.is_gt)\
               .then_inc(s["over"], 1)
            dve.wait_ge(s["over"], 1)
            dve.tensor_reduce(ntile[:, :], over[:, :, :], AX, ALU.add).then_inc(s["ntile"], 1)
            dve.wait_ge(s["ntile"], 1)
            dve.tensor_tensor(prod[:, :, :], ntile[:, :].unsqueeze(1).to_broadcast([1, E, E]), upto[:, :, :], ALU.mult)\
               .then_inc(s["prod"], 1)
            dve.tensor_scalar(jump[:, :], ntile[:, :], -float(ROWS), float(REGION), ALU.mult, ALU.add).then_inc(s["jump"], 1)
            dve.wait_ge(s["prod"], 1)
            dve.tensor_reduce(tile_end[:, :], prod[:, :, :], AX, ALU.add).then_inc(s["tile_end"], 1)
            dve.wait_ge(s["tile_end"], 1)
            dve.tensor_tensor(past[:, :, :], tile_no[:, :, :], tile_end[:, :].unsqueeze(1).to_broadcast([1, TILES, E]), ALU.is_ge)\
               .then_inc(s["past"], 1)
            dve.wait_ge(s["past"], 1)
            dve.wait_ge(s["jump"], 1)
            dve.tensor_reduce(t_expert[:, :], past[:, :, :], AX, ALU.add).then_inc(s["t_expert"], 1)
            dve.tensor_tensor(moved[:, :, :], past[:, :, :], jump[:, :].unsqueeze(1).to_broadcast([1, TILES, E]), ALU.mult)\
               .then_inc(s["moved"], 1)
            dve.wait_ge(s["moved"], 1)
            dve.tensor_reduce(t_row[:, :], moved[:, :, :], AX, ALU.add).then_inc(s["t_row0"], 1)
            dve.wait_ge(s["t_row0"], 1)
            dve.scalar_tensor_tensor(t_row[:, :], tile_no[:, :, 0], float(ROWS), t_row[:, :], ALU.mult, ALU.add)\
               .then_inc(s["t_row1"], 1)
            dve.wait_ge(s["t_row1"], 1)
            dve.tensor_scalar(tile_expert[:, :], t_expert[:, :], float(E - 1), None, ALU.min)
            dve.tensor_scalar(tile_row[:, :], t_row[:, :], float(SPARE), None, ALU.min).then_inc(s["table"], 1)

            dve.wait_ge(s["hb_ps"], 1)
            dve.wait_ge(s["b1T"], 1)
            dve.tensor_tensor(h_bias[:, :], ps_upd[:, 0:E * C], b1T[:, :], ALU.add).then_inc(s["h_bias"], 1)
            dve.wait_ge(s["w1h"], 1)
            for e in range(E):
                last = dve.scalar_tensor_tensor(W1l[:, e * HID:(e + 1) * HID], W1_sb[:, e, :], gain[:, e:e + 1],
                                                W1h[:, e * HID:(e + 1) * HID], ALU.mult, ALU.subtract)
            last.then_inc(s["w1l"], 1)
            dve.wait_ge(s["w2h"], 1)
            dve.scalar_tensor_tensor(W2l[:, :], W2_sb[:, :, :, :].rearrange("p e c d -> p (e c d)"), WSCALE, W2h[:, :],
                                     ALU.mult, ALU.subtract).then_inc(s["w2l"], 1)
            dve.wait_ge(s["ex"], 1)
            dve.tensor_scalar(ex1[:, :], ex[:, :], 1.0, None, ALU.add).then_inc(s["ex1"], 1)
            dve.wait_ge(s["ex1"], 1)
            dve.reciprocal(weight[:, 0, :], ex1[:, :]).then_inc(s["wt0"], 1)
            dve.wait_ge(s["wt0"], 1)
            dve.tensor_tensor(weight[:, 1, :], weight[:, 0, :], ex[:, :], ALU.mult).then_inc(s["weight"], 1)

            def low(t, q):
                dve.wait_ge(s["tTh"], t + 1)
                dve.tensor_tensor(tTl[q][:, :], ps_tT[q][:, 0:ROWS], tTh[q][:, :], ALU.subtract).then_inc(s["tTl"], 1)
                loaded(dve, "tin", t, q)
                dve.tensor_copy(result_row[:, at(t), :].rearrange("p o u -> p (o u)"),
                                tin[q][:, :, D:RW].bitcast(u32).rearrange("p u a -> p (u a)")).then_inc(s["result_row"], 1)

            def split(t, q):
                for half in range(2):
                    part = slice(half * (C // 2), (half + 1) * (C // 2))
                    dve.wait_ge(s["gel"], 2 * t + half + 1)
                    dve.tensor_copy(gelh[q][:, part, :], gel[q][:, part, :]).then_inc(s["gelh"], 1)
                    dve.wait_ge(s["gelh"], 2 * t + half + 1)
                    dve.tensor_tensor(gell[q][:, part, :], gel[q][:, part, :], gelh[q][:, part, :], ALU.subtract)\
                       .then_inc(s["gell"], 1)

            def finish(t, q):
                e = dve.value_load(tile_expert[0:1, at(t)], min_val=0, max_val=E - 1)
                dve.wait_ge(s["y_ps"], t + 1)
                if later(t, 2):
                    dve.wait_ge(s[f"sent{q}"], 16 * SUB * (t // 2) if isinstance(t, int) else 8 * SUB * (t - q))
                dve.tensor_copy(send_to[q][:, :], result_row[:, at(t), :].rearrange("p o u -> p (o u)"))
                dve.scalar_tensor_tensor(y[q][:, :, :], ps_y[q][:, 0:SUB * D].rearrange("p (u d) -> p u d", u=SUB), 1.0 / WSCALE,
                                         b2_all[:, bass.ds(e, 1), :].to_broadcast([P, SUB, D]), ALU.mult, ALU.add)\
                   .then_inc(s["y"], 1)

            def tile_step(n, q):
                if has(n, 2, TILES):
                    finish(n - 2, q)
                if has(n, -1, TILES):
                    low(n + 1, 1 - q)
                if has(n, 0, TILES):
                    split(n, q)

            dve.wait_ge(s["w_in"], 16 * len(weight_loads))
            low(0, 0)
            tile_steps(dve, tile_step)

            def combine(b, q):
                loaded(dve, "yk", b, q, 16 * K)
                dve.wait_ge(s["weight"], 1)
                if later(b, 1):
                    dve.wait_ge(s["total"], b)
                for t in range(T):
                    last = dve.scalar_tensor_tensor(first[:, t, :], yk[q][:, 0, t, :], weight[:, 0, at(b * T + t)], block_x2(b, t),
                                                    ALU.mult, ALU.add)
                last.then_inc(s["first"], 1)
                dve.wait_ge(s["first"], b + 1)
                dve.wait_ge(s["second"], b + 1)
                if later(b, 2):
                    dve.wait_ge(s[f"stored{q}"], 16 * (b // 2) if isinstance(b, int) else 8 * (b - q))
                dve.tensor_tensor(total[q][:, :, :], first[:, :, :], second[q][:, :, :], ALU.add).then_inc(s["total"], 1)

            combine(0, 0)
            combine(1, 1)
            with dve.Fori(2, B - 1, 2) as b:
                combine(b, 0)
                combine(b + 1, 1)


_INS = ["x", "adj", "L0_gnn_W_msg", "L0_gnn_W_upd", "L0_gnn_bias", "L0_ffn_Wr", "L0_ffn_br", "L0_ffn_ln_g", "L0_ffn_ln_b",
        "L0_ffn_W1", "L0_ffn_b1", "L0_ffn_W2", "L0_ffn_b2"]


def kernel(**inputs):
    import numpy as _np
    import concourse.bacc as _bacc
    from concourse import mybir as _mybir
    from concourse.bass_utils import run_bass_kernel_spmd as _run

    nc = _bacc.Bacc("TRN2", target_bir_lowering=False, num_devices=1)
    arrays, args = {}, []
    for name in _INS:
        a = _np.ascontiguousarray(inputs[name])
        arrays[f"in_{name}_dram"] = a
        args.append(nc.dram_tensor(f"in_{name}_dram", a.shape, _mybir.dt.from_np(a.dtype), kind="ExternalInput").ap())
    args.append(nc.dram_tensor("out_dram", (16, 512, 128), _mybir.dt.float32, kind="ExternalOutput").ap())
    graph_then_experts_kernel(nc, *args)
    r = _run(nc, [arrays], core_ids=[0])
    return r.results[0]["out_dram"]
```

```python
import concourse.bass as bass
from concourse import mybir
from contextlib import ExitStack


def graph_then_experts_kernel(nc, x, adj, W_msg, W_upd, bias, Wr, br, ln_g, ln_b, W1, b1, W2, b2, out):
    fp32, fp16, i32, u32 = mybir.dt.float32, mybir.dt.float16, mybir.dt.int32, mybir.dt.uint32
    ALU = mybir.AluOpType
    ACT = mybir.ActivationFunctionType
    AX = mybir.AxisListType.X

    P = 128
    B, N, D = x.shape
    E, _, HID = W1.shape
    K = 2
    T = N // P
    C = HID // P
    NODES = B * N
    H = B // 2
    Q = 2 * T
    assert H == E
    ROWS = 512
    SUB = ROWS // P
    REGION = NODES + ROWS
    TILES = K * NODES // ROWS + E - 1
    SPARE = E * REGION
    RW = D + 1
    NOWHERE = 1 << 20
    EPS = 1e-5
    WSCALE = 64.0
    FAR = 3e38

    rows = nc.dram_tensor("expert_rows", [SPARE + ROWS, RW], fp32, kind="Internal").ap()
    results = nc.dram_tensor("expert_results", [K * NODES, D], fp32, kind="Internal").ap()

    ctx = ExitStack()
    with ctx:
        def sb(name, shape, dt=fp32):
            return ctx.enter_context(nc.sbuf_tensor(name, shape, dt))

        def pb(name, shape, dt=fp32):
            return ctx.enter_context(nc.psum_tensor(name, shape, dt))

        def sem(name):
            return ctx.enter_context(nc.semaphore(name))

        ident = sb("ident", [P, P])
        ident16 = sb("ident16", [P, P], fp16)
        earlier = sb("earlier", [P, P], fp16)
        ones16 = sb("ones16", [P, P], fp16)
        held = sb("held", [P, 1], fp16)
        eps_col = sb("eps_col", [P, 1])
        expert_no = sb("expert_no", [P, Q, E])
        expert_no8 = sb("expert_no8", [P, Q, E])
        result_rows = sb("result_rows", [P, H, K, Q], i32)
        br_all = sb("br_all", [P, E])
        bias_row = sb("bias_row", [1, D])
        bias_h = sb("bias_h", [1, D], fp16)
        bias_l = sb("bias_l", [1, D], fp16)
        b2_all = sb("b2_all", [P, E, D])
        pad_rows = sb("pad_rows", [P, SUB, RW])
        Wm_sb = sb("Wm_sb", [D, D])
        Wu_sb = sb("Wu_sb", [D, D])
        Wr_sb = sb("Wr_sb", [D, E])
        Wrh = sb("Wrh", [D, E], fp16)
        Wrl = sb("Wrl", [D, E], fp16)

        W1_in = [sb(f"W1_in{q}", [D, HID]) for q in range(2)]
        W2_in = [sb(f"W2_in{q}", [P, C, D]) for q in range(2)]
        W1h = sb("W1h", [D, E * HID], fp16)
        W1l = sb("W1l", [D, E * HID], fp16)
        W2h = sb("W2h", [P, E * C * D], fp16)
        W2l = sb("W2l", [P, E * C * D], fp16)
        gb_rows = sb("gb_rows", [2 * E, D])
        b1_rows = sb("b1_rows", [E * C, P])
        gain = sb("gain", [D, E])
        offset = sb("offset", [D, E])
        b1T = sb("b1T", [P, E * C])
        h_bias = sb("h_bias", [P, E * C])

        x2 = sb("x2", [P, H, Q, D])
        adj_int = [sb(f"adj_int{g}", [P, T, N], i32) for g in range(2)]
        adj16 = [[sb(f"adj16_{q}{g}", [P, T, N], fp16) for g in range(2)] for q in range(2)]
        xn = sb("xn", [P, Q, D])
        xnT = sb("xnT", [D, 2 * N])
        msgh = [sb(f"msgh{q}", [P, Q, D], fp16) for q in range(2)]
        msgl = [sb(f"msgl{q}", [P, Q, D], fp16) for q in range(2)]
        upd = [sb(f"upd{q}", [P, Q, D]) for q in range(2)]
        summed = sb("summed", [P, Q, D])
        row32 = sb("row32", [P, Q, D])
        row = [sb(f"row{q}", [P, K, Q, RW]) for q in range(2)]
        row16 = [row[q][:, 0, :, :].bitcast(fp16) for q in range(2)]
        rowT = sb("rowT", [D, 2, 2 * N], fp16)
        member = sb("member", [P, Q, E], fp16)
        dest = [sb(f"dest{q}", [P, K, Q], u32) for q in range(2)]
        stats = {w: sb(f"stats{w}", [P, Q, 6]) for w in "AB"}
        mean2 = {w: sb(f"mean2{w}", [P, Q]) for w in "AB"}
        gap = {w: sb(f"gap{w}", [P, Q]) for w in "AB"}
        spread = {w: sb(f"spread{w}", [P, Q]) for w in "AB"}
        gap_sq = {w: sb(f"gap_sq{w}", [P, Q]) for w in "AB"}
        dvar = {w: sb(f"dvar{w}", [P, Q]) for w in "AB"}
        sd = {w: sb(f"sd{w}", [P, Q]) for w in "AB"}
        rs = {w: sb(f"rs{w}", [P, Q]) for w in "AB"}
        shiftA = sb("shiftA", [P, Q])
        half_out = sb("half_out", [P, Q])
        dvar2 = sb("dvar2", [P, Q])
        sd2 = [sb(f"sd2{q}", [P, Q]) for q in range(2)]
        rs2 = sb("rs2", [P, Q])
        rsBoth = sb("rsBoth", [P, Q])
        meanB = sb("meanB", [P, Q])
        degm = sb("degm", [P, Q])
        degr = sb("degr", [P, Q])
        degw = sb("degw", [P, Q])
        lg0 = sb("lg0", [P, Q, E])
        lg = sb("lg", [P, Q, E])
        lg2 = sb("lg2", [P, Q, E])
        top = sb("top", [P, K, Q])
        hit = [sb(f"hit{k}", [P, Q, E]) for k in range(K)]
        key = [sb(f"key{k}", [P, Q, E]) for k in range(K)]
        chosen = [sb(f"chosen{k}", [P, Q]) for k in range(K)]
        onehot = sb("onehot", [P, K, Q, E])
        pos = sb("pos", [P, Q, E])
        picked = sb("picked", [P, K, Q, E])
        free_row = sb("free_row", [P, E])
        margin = sb("margin", [P, H, Q])

        free_int = sb("free_int", [1, E], i32)
        count = sb("count", [1, E])
        steps32 = sb("steps32", [1, E, NODES // ROWS])
        over = sb("over", [1, E, NODES // ROWS])
        ntile = sb("ntile", [1, E])
        upto = sb("upto", [1, E, E])
        prod = sb("prod", [1, E, E])
        tile_end = sb("tile_end", [1, E])
        jump = sb("jump", [1, E])
        tile_no = sb("tile_no", [1, TILES, E])
        past = sb("past", [1, TILES, E])
        moved = sb("moved", [1, TILES, E])
        t_expert = sb("t_expert", [1, TILES])
        t_row = sb("t_row", [1, TILES])
        tile_expert = sb("tile_expert", [1, TILES], i32)
        tile_row = sb("tile_row", [1, TILES], i32)

        tin = [sb(f"tin{q}", [P, SUB, RW]) for q in range(2)]
        result_row = sb("result_row", [P, TILES, SUB], u32)
        tin16 = [tin[q][:, :, :].bitcast(fp16) for q in range(2)]
        tT = [sb(f"tT{q}", [D, 2, ROWS], fp16) for q in range(2)]
        gel = [adj_int[q][:, :, :].bitcast(fp32) for q in range(2)]
        gelh, gell = [adj16[q][0] for q in range(2)], [adj16[q][1] for q in range(2)]
        y = [sb(f"y{q}", [P, SUB, D]) for q in range(2)]
        send_to = [sb(f"send_to{q}", [P, SUB], u32) for q in range(2)]

        weight = sb("weight", [P, K, B * T])
        ex = sb("ex", [P, B * T])
        ex1 = sb("ex1", [P, B * T])
        yk = [gel[q][:, 0:K, :].rearrange("p k (t d) -> p k t d", t=T) for q in range(2)]
        second = [gel[q][:, K, :].rearrange("p (t d) -> p t d", t=T) for q in range(2)]
        first = sb("first", [P, T, D])
        total = [gel[q][:, K + 1, :].rearrange("p (t d) -> p t d", t=T) for q in range(2)]

        bank = [pb(f"bank{i}", [P, 512]) for i in range(8)]
        ps_sum, ps_msg = bank[0:2], bank[2:4]
        ps_upd, ps_xnT, ps_rowT, ps_small = bank[4:8]
        ps_logit = ps_small[:, 0:Q * E]
        ps_rank = ps_small[:, Q * E:2 * Q * E]
        ps_placed = ps_small[:, 2 * Q * E:2 * Q * E + E]
        ps_deg = ps_small[:, 256:256 + Q]
        ps_hb = ps_small[:, 288:288 + C]
        ps_h = [bank[c][:, :] for c in range(C)]
        ps_tT = [bank[4 + q][:, :].bitcast(fp16) for q in range(2)]
        ps_y = bank[6:8]

        names = """x_in0 x_in1 adj_in0 adj_in1 const_in gains_in w_in0 w_in1
            const_id0 const_id const_id16 wr_high wr_low bias_high bias_low const_tri0 const_tri const_pool const_dve
            bnA levelA gap_sqA dvarA sdA rsA shiftA xn xnT_ps xnT msg_ps upd_ps msg_high msg_low upd adj16
            sum_ps degm degr degw summed x2 bnB levelB gap_sqB dvarB sdB rsB half_out dvar2 sd2 rs2 rsBoth row32 row_high row_low
            rowT_ps rowT row_copied0 row_copied1 logit_ps lg0 lg lg2 member rank_ps pos picked dest free_row
            top1 hit1 key1 chosen1 onehot1 top2 hit2 key2 chosen2 onehot2 scattered0 scattered1
            gbT_ps gain offset b1T h_bias w1h w1l w2h w2l
            cnt over ntile prod tile_end jump past texp t_expert moved t_row0 t_row1 table free_int
            pads held
            tin0 tin1 tT_ps tT result_row h_ps gel gelh gell y_ps y sent0 sent1
            ex ex1 wt0 weight yk0 yk1 second first total stored0 stored1""".split()
        s = {n: sem(n) for n in names}

        const_loads = [(Wm_sb[:, :], W_msg), (Wu_sb[:, :], W_upd),
                       (bias_row[:, :], bias.rearrange("(a n) -> a n", a=1)), (Wr_sb[:, :], Wr),
                       (br_all[:, :], br.rearrange("(a n) -> a n", a=1).broadcast_to([P, E]))]
        gain_loads = [(gb_rows[0:E, :], ln_g), (gb_rows[E:2 * E, :], ln_b),
                      (b1_rows[:, :], b1.rearrange("e (c p) -> (e c) p", p=P)),
                      (b2_all[:, :, :], b2.rearrange("(a e) d -> a e d", a=1).broadcast_to([P, E, D]))]

        block = ctx.enter_context(nc.Block())

        def pair_steps(eng, step):
            for n in range(4):
                step(n, n % 2)
            with eng.Fori(4, H - 1, 2) as n:
                step(n, 0)
                step(n + 1, 1)
            for n in (H, H + 1, H + 2):
                step(n, n % 2)

        def tile_steps(eng, step):
            for n in range(4):
                step(n, n % 2)
            with eng.Fori(4, TILES - 2, 2) as n:
                step(n, 0)
                step(n + 1, 1)
            for n in (TILES - 1, TILES, TILES + 1):
                step(n, n % 2)

        def has(n, lag, count=H):
            return not isinstance(n, int) or 0 <= n - lag < count

        def later(n, least):
            return not isinstance(n, int) or n >= least

        def loaded(eng, name, n, q, each=16):
            eng.wait_ge(s[f"{name}{q}"], each * (n // 2 + 1) if isinstance(n, int) else (n - q) * (each // 2) + each)

        def scattered(p, q):
            return 16 * K * Q * (p // 2) if isinstance(p, int) else 8 * K * Q * (p - q)

        def part_of(e):
            return slice(e * HID, (e + 1) * HID) if isinstance(e, int) else bass.ds(e * HID, HID)

        def at(n):
            return slice(n, n + 1) if isinstance(n, int) else bass.ds(n, 1)

        def pair_of(p):
            return slice(2 * p, 2 * p + 2) if isinstance(p, int) else bass.ds(2 * p, 2)

        def pair_x2(p, g=None):
            part = slice(0, Q) if g is None else slice(g * T, (g + 1) * T)
            return x2[:, at(p), part, :].rearrange("p o t d -> p (o t) d")

        def block_x2(p, t):
            return x2[:, at(p), t, :].rearrange("p o d -> p (o d)")

        def graph(tensor, b):
            return tensor[at(b)]

        @block.sync
        def _(sp):
            def step(n, q):
                if has(n, 0):
                    if later(n, 2):
                        sp.wait_ge(s["dvarA"], n - 1)
                    sp.dma_start(x2[:, at(n), :, :].rearrange("p o t d -> p (o t) d"),
                                 x[pair_of(n)].rearrange("g (t p) d -> p (g t) d", p=P)).then_inc(s[f"x_in{q}"], 16)
                    for g in range(2):
                        if later(n, 1):
                            sp.wait_ge(s["adj16"], 2 * n + g - 1)
                        sp.dma_start(adj_int[g][:, :, :], adj[at(2 * n + g)].rearrange("o (t p) n -> p (o t) n", p=P))\
                            .then_inc(s[f"adj_in{g}"], 16)
                    if later(n, 2):
                        sp.wait_ge(s["w1l"], n - 1)
                        sp.wait_ge(s["w2l"], n - 1)
                        sp.wait_ge(s["sum_ps"], n - 1)
                    sp.dma_start(W1_in[q][:, :], W1[at(n)].rearrange("o d h -> d (o h)")).then_inc(s[f"w_in{q}"], 16)
                    sp.dma_start(W2_in[q][:, :, :], W2[at(n)].rearrange("o (c h) d -> h (o c) d", h=P)).then_inc(s[f"w_in{q}"], 16)
                if has(n, 3):
                    sp.wait_ge(s["row_low"], 2 * (n - 3) + 2)
                    sp.dma_start(row[1 - q][:, 1, :, 0:D], row[1 - q][:, 0, :, 0:D]).then_inc(s[f"row_copied{1 - q}"], 16)

            pair_steps(sp, step)
            sp.dma_start(*gain_loads[3]).then_inc(s["gains_in"], 16)

            sp.wait_ge(s["const_pool"], 1)
            sp.wait_ge(s["free_int"], 1)
            for e in range(E):
                start = sp.value_load(free_int[0:1, e:e + 1], min_val=e * REGION, max_val=e * REGION + NODES)
                sp.dma_start(rows[bass.ds(start, ROWS), :].rearrange("(s p) w -> p s w", p=P), pad_rows[:, :, :]).then_inc(s["pads"], 16)
            sp.dma_start(rows[SPARE:SPARE + ROWS, :].rearrange("(s p) w -> p s w", p=P), pad_rows[:, :, :]).then_inc(s["pads"], 16)

            sp.wait_ge(s["pads"], 16 * (E + 1))
            for q in range(2):
                sp.wait_ge(s[f"scattered{q}"], 16 * K * Q * (H // 2))
            sp.wait_ge(s["table"], 1)

            def load_tile(t, q):
                start = sp.value_load(tile_row[0:1, at(t)], min_val=0, max_val=SPARE)
                if later(t, 2):
                    sp.wait_ge(s["tT_ps"], t - 1)
                    sp.wait_ge(s["result_row"], t - 1)
                sp.dma_start(tin[q][:, :, :], rows[bass.ds(start, ROWS), :].rearrange("(s p) w -> p s w", p=P)).then_inc(s[f"tin{q}"], 16)

            load_tile(0, 0)
            load_tile(1, 1)
            with sp.Fori(2, TILES - 2, 2) as t:
                load_tile(t, 0)
                load_tile(t + 1, 1)
            load_tile(TILES - 1, 0)

            for q in range(2):
                sp.wait_ge(s[f"sent{q}"], 16 * SUB * ((TILES + 1 - q) // 2))
            by_graph = results.rearrange("(k b t p) d -> b k p t d", k=K, b=B, p=P)

            def load_results(b, q):
                if later(b, 2):
                    sp.wait_ge(s["first"], b - 1)
                    sp.wait_ge(s["second"], b - 1)
                for k in range(K):
                    sp.dma_start(yk[q][:, k, :, :], graph(by_graph, b)[:, k].rearrange("o p t d -> p (o t) d")).then_inc(s[f"yk{q}"], 16)

            load_results(0, 0)
            load_results(1, 1)
            with sp.Fori(2, B - 1, 2) as b:
                load_results(b, 0)
                load_results(b + 1, 1)

        @block.gpsimd
        def _(pool):
            pool.memset(ident[:, :], 0.0).then_inc(s["const_id0"], 1)
            pool.wait_ge(s["const_id0"], 1)
            pool.affine_select(out=ident[:, :], in_=ident[:, :], compare_op=ALU.not_equal, fill=1.0,
                               base=0, pattern=[[-1, P]], channel_multiplier=1).then_inc(s["const_id"], 1)
            pool.wait_ge(s["const_id"], 1)
            pool.tensor_copy(ident16[:, :], ident[:, :]).then_inc(s["const_id16"], 1)
            pool.memset(earlier[:, :], 0.0).then_inc(s["const_tri0"], 1)
            pool.wait_ge(s["const_tri0"], 1)
            pool.affine_select(out=earlier[:, :], in_=earlier[:, :], compare_op=ALU.is_ge, fill=1.0,
                               base=0, pattern=[[-1, P]], channel_multiplier=1).then_inc(s["const_tri"], 1)
            pool.memset(ones16[:, :], 1.0)
            pool.memset(upto[:, :, :], 0.0).then_inc(s["const_tri0"], 1)
            pool.wait_ge(s["const_tri0"], 2)
            pool.affine_select(out=upto[:, :, :], in_=upto[:, :, :], compare_op=ALU.is_gt, fill=1.0,
                               base=0, pattern=[[-1, E], [1, E]], channel_multiplier=0)
            pool.iota(expert_no[:, :, :], pattern=[[0, Q], [1, E]], base=0, channel_multiplier=0,
                      allow_small_or_imprecise_dtypes=True)
            pool.iota(expert_no8[:, :, :], pattern=[[0, Q], [1, E]], base=E, channel_multiplier=0,
                      allow_small_or_imprecise_dtypes=True)
            pool.iota(result_rows[:, :, :, :], pattern=[[2 * N, H], [NODES, K], [P, Q]], base=0, channel_multiplier=1)
            pool.iota(free_row[:, :], pattern=[[REGION, E]], base=0, channel_multiplier=0,
                      allow_small_or_imprecise_dtypes=True)
            pool.iota(steps32[:, :, :], pattern=[[0, E], [ROWS, NODES // ROWS]], base=0, channel_multiplier=0,
                      allow_small_or_imprecise_dtypes=True)
            pool.iota(tile_no[:, :, :], pattern=[[1, TILES], [0, E]], base=0, channel_multiplier=0,
                      allow_small_or_imprecise_dtypes=True)
            pool.memset(pad_rows[:, :, 0:D], 0.0)
            pool.memset(pad_rows[:, :, D:RW].bitcast(i32), NOWHERE)
            pool.memset(eps_col[:, :], EPS).then_inc(s["const_pool"], 1)

            def hold(before):
                if later(before, 1):
                    pool.wait_ge(s["held"], before)
                pool.tensor_tensor(held[:, :], ones16[:, 0:1], ones16[:, 0:1], ALU.mult).then_inc(s["held"], 1)

            def scatter(n, q):
                if not has(n, 3):
                    return
                p, q = n - 3, 1 - q
                pool.wait_ge(s["dest"], p + 1)
                loaded(pool, "row_copied", p, q)
                hold(p)
                for k in range(K):
                    for t in range(Q):
                        pool.indirect_dma_start(rows, bass.IndirectOffsetOnAxis(ap=dest[q][:, k, t:t + 1], axis=0),
                                                row[q][:, k, t, :], None).then_inc(s[f"scattered{q}"], 16)

            pair_steps(pool, scatter)

            def send(t, q):
                pool.wait_ge(s["y"], t + 1)
                hold(t + H)
                for u in range(SUB):
                    idx = send_to[q][:, u:u + 1]
                    pool.indirect_dma_start(results, bass.IndirectOffsetOnAxis(ap=idx, axis=0), y[q][:, u, :], None,
                                            bounds_check=K * NODES - 1, oob_is_err=False).then_inc(s[f"sent{q}"], 16)

            with pool.Fori(0, TILES - 2, 2) as t:
                send(t, 0)
                send(t + 1, 1)
            send(TILES - 1, 0)

        @block.tensor
        def _(pe):
            pe.wait_ge(s["const_id"], 1)
            pe.wait_ge(s["const_tri"], 1)
            pe.wait_ge(s["const_pool"], 1)
            pe.wait_ge(s["const_in"], 16 * (3 + len(const_loads)))
            pe.transpose(ps_rowT[:, 0:2 * E], gb_rows[:, :], ident[0:2 * E, 0:2 * E])
            pe.transpose(ps_rowT[:, 2 * E:2 * E + E * C], b1_rows[:, :], ident[0:E * C, 0:E * C]).then_inc(s["gbT_ps"], 1)
            pe.wait_ge(s["const_id16"], 1)
            pe.wait_ge(s["wr_low"], 1)
            pe.wait_ge(s["bias_low"], 1)
            pe.wait_ge(s["b1T"], 1)

            def turn_rows(p, g, q):
                pe.wait_ge(s["row_low"], 2 * p + g + 1)
                if g or later(p, 1):
                    pe.wait_ge(s["rowT"], 2 * p + g)
                to = ps_rowT[:, :].bitcast(fp16)
                for part in range(2):
                    for t in range(T):
                        a = part * N + t * P
                        last = pe.transpose(to[:, a:a + P], row16[q][:, g * T + t, part * D:(part + 1) * D], ident16[:, :])
                last.then_inc(s["rowT_ps"], 1)

            def turn_nodes(p, g):
                pe.wait_ge(s["xn"], 2 * p + g + 1)
                if g or later(p, 1):
                    pe.wait_ge(s["xnT"], 2 * p + g)
                for t in range(T):
                    last = pe.transpose(ps_xnT[:, t * P:(t + 1) * P], xn[:, g * T + t, :], ident[:, :])
                last.then_inc(s["xnT_ps"], 1)

            def logits(p):
                pe.wait_ge(s["rowT"], 2 * p + 2)
                for t in range(Q):
                    to = ps_logit[:, t * E:(t + 1) * E]
                    high, low = (rowT[:, part, t * P:(t + 1) * P] for part in range(2))
                    pe.matmul(to, high, Wrh[:, :], start=True, stop=False)
                    pe.matmul(to, high, Wrl[:, :], start=False, stop=False)
                    last = pe.matmul(to, low, Wrh[:, :], start=False, stop=True)
                last.then_inc(s["logit_ps"], 1)

            def messages(p, g):
                pe.wait_ge(s["xnT"], 2 * p + g + 1)
                if later(p, 1):
                    pe.wait_ge(s["msg_low"], 2 * p + g - 1)
                for t in range(T):
                    a = g * N + t * P
                    last = pe.matmul(ps_msg[g][:, t * D:(t + 1) * D], xnT[:, a:a + P], Wm_sb[:, :], start=True, stop=True)
                last.then_inc(s["msg_ps"], 1)

            def updates(p, g):
                if g or later(p, 1):
                    pe.wait_ge(s["upd"], 2 * p + g)
                for t in range(T):
                    a = g * N + t * P
                    to = ps_upd[:, t * D:(t + 1) * D]
                    pe.matmul(to, xnT[:, a:a + P], Wu_sb[:, :], start=True, stop=False)
                    pe.matmul(to, ones16[0:1, :], bias_h[:, :], start=False, stop=False)
                    last = pe.matmul(to, ones16[0:1, :], bias_l[:, :], start=False, stop=True)
                last.then_inc(s["upd_ps"], 1)

            def rank(p):
                pe.wait_ge(s["member"], p + 1)
                pe.matmul(ps_rank[:, :], earlier[:, :], member[:, :, :].rearrange("p t e -> p (t e)"), start=True, stop=False)
                for k in range(1, Q):
                    pe.matmul(ps_rank[:, k * E:Q * E], ones16[:, :], member[:, 0:Q - k, :].rearrange("p t e -> p (t e)"),
                              start=False, stop=(k == Q - 1))
                for t in range(Q):
                    last = pe.matmul(ps_placed[:, :], ones16[:, :], member[:, t, :], start=(t == 0), stop=(t == Q - 1))
                last.then_inc(s["rank_ps"], 1)

            def neighbours(p, g, q):
                pe.wait_ge(s["msg_low"], 2 * p + g + 1)
                pe.wait_ge(s["adj16"], 2 * p + g + 1)
                if later(p, 1):
                    pe.wait_ge(s["summed"], p)
                for j in range(T):
                    to = ps_sum[g][:, j * D:(j + 1) * D]
                    for i in range(T):
                        pe.matmul(to, adj16[q][g][:, i, j * P:(j + 1) * P], msgh[q][:, g * T + i, :], start=(i == 0), stop=False)
                        pe.matmul(to, adj16[q][g][:, i, j * P:(j + 1) * P], msgl[q][:, g * T + i, :],
                                  start=False, stop=(i == T - 1))

            def degrees(p, q):
                for c in range(C):
                    pe.matmul(ps_hb[:, c:c + 1], W1_in[q][:, c * P:(c + 1) * P], offset[:, at(p)], start=True, stop=True)
                for g in range(2):
                    for j in range(T):
                        for i in range(T):
                            last = pe.matmul(ps_deg[:, g * T + j:g * T + j + 1], adj16[q][g][:, i, j * P:(j + 1) * P],
                                             ones16[:, 0:1], start=(i == 0), stop=(i == T - 1))
                last.then_inc(s["sum_ps"], 1)

            def step(n, q):
                for g in range(2):
                    if has(n, 3):
                        turn_rows(n - 3, g, 1 - q)
                    if has(n, 1):
                        turn_nodes(n - 1, g)
                if has(n, 3):
                    if has(n, 2):
                        pe.wait_ge(s["degw"], n - 1)
                        pe.wait_ge(s["h_bias"], n - 1)
                    logits(n - 3)
                if has(n, 1):
                    messages(n - 1, 0)
                    messages(n - 1, 1)
                    updates(n - 1, 0)
                    updates(n - 1, 1)
                if has(n, 3):
                    rank(n - 3)
                if has(n, 1):
                    neighbours(n - 1, 0, 1 - q)
                    neighbours(n - 1, 1, 1 - q)
                    if has(n, 3):
                        pe.wait_ge(s["pos"], n - 2)
                        pe.wait_ge(s["free_row"], n - 2)
                    elif has(n, 2):
                        pe.wait_ge(s["degw"], n - 1)
                        pe.wait_ge(s["h_bias"], n - 1)
                    loaded(pe, "w_in", n - 1, 1 - q, 32)
                    degrees(n - 1, 1 - q)

            pair_steps(pe, step)

            pe.wait_ge(s["table"], 1)
            pe.wait_ge(s["h_bias"], H)
            pe.wait_ge(s["upd"], B)
            pe.wait_ge(s["rowT"], B)
            pe.wait_ge(s["summed"], H)
            pe.wait_ge(s["w1l"], E)
            pe.wait_ge(s["w2l"], E)

            def expert(t):
                return pe.value_load(tile_expert[0:1, at(t)], min_val=0, max_val=E - 1)

            def turn(t, q):
                loaded(pe, "tin", t, q)
                if later(t, 2):
                    pe.wait_ge(s["tT"], t - 1)
                for part in range(2):
                    for u in range(SUB):
                        at_ = part * ROWS + u * P
                        last = pe.transpose(ps_tT[q][:, at_:at_ + P], tin16[q][:, u, part * D:(part + 1) * D], ident16[:, :])
                last.then_inc(s["tT_ps"], 1)

            def hidden(t, q, e):
                pe.wait_ge(s["tT"], t + 1)
                for c in range(C):
                    if c % 2 == 0 and later(t, 1):
                        pe.wait_ge(s["gel"], 2 * t + c // 2 - 1)
                    w = bass.ds(e * HID + c * P, P)
                    high, low = tT[q][:, 0, :], tT[q][:, 1, :]
                    pe.matmul(ps_h[c], W1h[:, w], high, start=True, stop=False)
                    pe.matmul(ps_h[c], W1h[:, w], low, start=False, stop=False)
                    pe.matmul(ps_h[c], W1l[:, w], high, start=False, stop=True).then_inc(s["h_ps"], 1)

            def output(t, q, e):
                if later(t, 2):
                    pe.wait_ge(s["y"], t - 1)
                for u in range(SUB):
                    to = ps_y[q][:, u * D:(u + 1) * D]
                    for c in range(C):
                        if u == 0 and c % 2 == 0:
                            pe.wait_ge(s["gell"], 2 * t + c // 2 + 1)
                        w = bass.ds(e * C * D + c * D, D)
                        gh = gelh[q][:, c, u * P:(u + 1) * P]
                        gl = gell[q][:, c, u * P:(u + 1) * P]
                        pe.matmul(to, gh, W2h[:, w], start=(c == 0), stop=False)
                        pe.matmul(to, gh, W2l[:, w], start=False, stop=False)
                        last = pe.matmul(to, gl, W2h[:, w], start=False, stop=(c == C - 1))
                last.then_inc(s["y_ps"], 1)

            def tile_step(n, q):
                if has(n, -1, TILES):
                    turn(n + 1, 1 - q)
                if has(n, 0, TILES):
                    hidden(n, q, expert(n))
                if has(n, 1, TILES):
                    output(n - 1, 1 - q, expert(n - 1))

            turn(0, 0)
            tile_steps(pe, tile_step)

        @block.scalar
        def _(act):
            for dst, src in gain_loads[0:3] + const_loads:
                act.dma_start(dst, src).then_inc(s["const_in"], 16)
            act.wait_ge(s["gbT_ps"], 1)
            act.mul(gain[:, :], ps_rowT[:, 0:E], WSCALE).then_inc(s["gain"], 1)
            act.activation(offset[:, :], ps_rowT[:, E:2 * E], ACT.Copy).then_inc(s["offset"], 1)
            act.activation(b1T[:, :], ps_rowT[:, 2 * E:2 * E + E * C], ACT.Copy).then_inc(s["b1T"], 1)
            act.wait_ge(s["const_pool"], 1)
            act.wait_ge(s["gain"], 1)

            def nodes(p):
                act.wait_ge(s["shiftA"], p + 1)
                if later(p, 1):
                    act.wait_ge(s["xnT_ps"], 2 * p)
                for g in range(2):
                    for t in range(g * T, (g + 1) * T):
                        last = act.activation(xn[:, t, :], block_x2(p, t), ACT.Identity, bias=shiftA[:, t:t + 1],
                                              scale=rs["A"][:, t:t + 1])
                    last.then_inc(s["xn"], 1)

            def turned_rows(p, g):
                act.wait_ge(s["rowT_ps"], 2 * p + g + 1)
                if g == 0 and later(p, 1):
                    act.wait_ge(s["logit_ps"], p)
                act.activation(rowT[:, :, g * N:(g + 1) * N], ps_rowT[:, :].bitcast(fp16).rearrange("p (a n) -> p a n", a=2), ACT.Copy)\
                   .then_inc(s["rowT"], 1)

            def turned_nodes(p, g):
                act.wait_ge(s["xnT_ps"], 2 * p + g + 1)
                if g == 0 and later(p, 1):
                    act.wait_ge(s["upd_ps"], 2 * p)
                act.activation(xnT[:, g * N:(g + 1) * N], ps_xnT[:, :], ACT.Copy).then_inc(s["xnT"], 1)

            def convert(p, g, q):
                act.wait_ge(s[f"adj_in{g}"], 16 * (p + 1))
                if later(p, 2):
                    act.wait_ge(s["sum_ps"], p - 1)
                act.activation(adj16[q][g][:, :, :], adj_int[g][:, :, :], ACT.Copy).then_inc(s["adj16"], 1)

            def root(p, w):
                act.wait_ge(s[f"dvar{w}"], p + 1)
                if later(p, 1):
                    act.wait_ge(s[f"rs{w}"], p)
                act.activation(sd[w][:, :], dvar[w][:, :], ACT.Sqrt, scale=1.0 / D, bias=eps_col[:, :]).then_inc(s[f"sd{w}"], 1)

            def root2(p, q):
                act.wait_ge(s["dvar2"], p + 1)
                act.activation(sd2[q][:, :], dvar2[:, :], ACT.Sqrt, scale=1.0 / D, bias=eps_col[:, :]).then_inc(s["sd2"], 1)

            def high_messages(p, g, q):
                part = slice(g * T, (g + 1) * T)
                act.wait_ge(s["msg_ps"], 2 * p + g + 1)
                act.activation(msgh[q][:, part, :], ps_msg[g][:, :].rearrange("p (t d) -> p t d", t=T), ACT.Copy)\
                   .then_inc(s["msg_high"], 1)

            def updates(p, g, q):
                part = slice(g * T, (g + 1) * T)
                act.wait_ge(s["upd_ps"], 2 * p + g + 1)
                if g == 0 and later(p, 2):
                    act.wait_ge(s["summed"], p - 1)
                act.activation(upd[q][:, part, :], ps_upd[:, :].rearrange("p (t d) -> p t d", t=T), ACT.Copy).then_inc(s["upd"], 1)

            def high_rows(p, q):
                act.wait_ge(s["row32"], p + 1)
                if later(p, 2):
                    act.wait_ge(s[f"scattered{q}"], scattered(p, q))
                act.activation(row16[q][:, :, 0:D], row32[:, :, :], ACT.Copy).then_inc(s["row_high"], 1)

            def high_weights(e, q):
                loaded(act, "w_in", e, q, 32)
                act.activation(W1h[:, part_of(e)], W1_in[q][:, :], ACT.Copy, scale=gain[:, at(e)]).then_inc(s["w1h"], 1)
                act.activation(W2h[:, part_of(e)], W2_in[q][:, :, :].rearrange("p c d -> p (c d)"), ACT.Copy, scale=WSCALE)\
                   .then_inc(s["w2h"], 1)

            def step(n, q):
                if has(n, 1):
                    nodes(n - 1)
                for g in range(2):
                    if has(n, 3):
                        turned_rows(n - 3, g)
                    if has(n, 1):
                        turned_nodes(n - 1, g)
                if has(n, 0):
                    convert(n, 0, q)
                if has(n, 1):
                    for g in range(2):
                        high_messages(n - 1, g, 1 - q)
                    for g in range(2):
                        updates(n - 1, g, 1 - q)
                if has(n, 2):
                    root(n - 2, "B")
                if has(n, 0):
                    convert(n, 1, q)
                if has(n, 1):
                    high_weights(n - 1, 1 - q)
                if has(n, 2):
                    root2(n - 2, q)
                if has(n, 0):
                    root(n, "A")
                if has(n, 2):
                    high_rows(n - 2, q)

            pair_steps(act, step)

            act.wait_ge(s["member"], H)
            act.activation(ex[:, :], margin[:, :, :].rearrange("p b t -> p (b t)"), ACT.Exp).then_inc(s["ex"], 1)

            act.wait_ge(s["h_bias"], E)
            act.wait_ge(s["table"], 1)

            def turned(t, q):
                act.wait_ge(s["tT_ps"], t + 1)
                if later(t, 2):
                    act.wait_ge(s["h_ps"], C * (t - 1))
                act.activation(tT[q][:, :, :].rearrange("p a r -> p (a r)"), ps_tT[q], ACT.Copy).then_inc(s["tT"], 1)

            def gelu(t, q):
                e = act.value_load(tile_expert[0:1, at(t)], min_val=0, max_val=E - 1)
                for c in range(C):
                    act.wait_ge(s["h_ps"], C * t + c + 1)
                    if c % 2 == 0 and later(t, 2):
                        act.wait_ge(s["gell"], 2 * (t - 2) + c // 2 + 1)
                    last = act.activation(gel[q][:, c, :], ps_h[c], ACT.Gelu, bias=h_bias[:, bass.ds(e * C + c, 1)],
                                          scale=1.0 / WSCALE)
                    if c % 2:
                        last.then_inc(s["gel"], 1)

            def tile_step(n, q):
                if has(n, -1, TILES):
                    turned(n + 1, 1 - q)
                if has(n, 0, TILES):
                    gelu(n, q)

            turned(0, 0)
            tile_steps(act, tile_step)

            act.wait_ge(s["weight"], 1)

            def weighted_second(b, q):
                loaded(act, "yk", b, q, 16 * K)
                if later(b, 2):
                    act.wait_ge(s["total"], b - 1)
                for t in range(T):
                    last = act.activation(second[q][:, t, :], yk[q][:, 1, t, :], ACT.Copy, scale=weight[:, 1, at(b * T + t)])
                last.then_inc(s["second"], 1)

            def store(b, q):
                act.wait_ge(s["total"], b + 1)
                act.dma_start(graph(out, b).rearrange("o (t p) d -> p (o t) d", p=P), total[q][:, :, :]).then_inc(s[f"stored{q}"], 16)

            def pair(b):
                weighted_second(b + 1, 1)
                store(b, 0)
                weighted_second(b + 2, 0)
                store(b + 1, 1)

            weighted_second(0, 0)
            pair(0)
            with act.Fori(2, B - 3, 2) as b:
                pair(b)
            weighted_second(B - 1, 1)
            store(B - 2, 0)
            store(B - 1, 1)
            for q in range(2):
                act.wait_ge(s[f"stored{q}"], 16 * (B // 2))

        @block.vector
        def _(dve):
            dve.wait_ge(s["const_pool"], 1)
            dve.wait_ge(s["const_in"], 16 * (3 + len(const_loads)))
            dve.tensor_copy(Wrh[:, :], Wr_sb[:, :]).then_inc(s["wr_high"], 1)
            dve.tensor_copy(bias_h[:, :], bias_row[:, :]).then_inc(s["bias_high"], 1)
            dve.wait_ge(s["wr_high"], 1)
            dve.tensor_tensor(Wrl[:, :], Wr_sb[:, :], Wrh[:, :], ALU.subtract).then_inc(s["wr_low"], 1)
            dve.wait_ge(s["bias_high"], 1)
            dve.tensor_tensor(bias_l[:, :], bias_row[:, :], bias_h[:, :], ALU.subtract).then_inc(s["bias_low"], 1)
            dve.wait_ge(s["b1T"], 1)

            def wide(a, n=E):
                return a.unsqueeze(2).to_broadcast([P, Q, n])

            def block_stats(p, w, q, blocks):
                dve.wait_ge(s["bias_low"], 1)
                if w == "B":
                    dve.wait_ge(s["x2"], 2 * p + 2)
                else:
                    loaded(dve, "x_in", p, q)
                for t in blocks:
                    last = dve.bn_stats(stats[w][:, t, :], block_x2(p, t))
                last.then_inc(s[f"bn{w}"], 1)

            def both_halves(p, w, waits):
                dve.wait_ge(s[f"bn{w}"], waits)
                dve.tensor_tensor(gap[w][:, :], stats[w][:, :, 1], stats[w][:, :, 4], ALU.subtract)
                dve.tensor_tensor(spread[w][:, :], stats[w][:, :, 2], stats[w][:, :, 5], ALU.add)
                dve.tensor_tensor(mean2[w][:, :], stats[w][:, :, 1], stats[w][:, :, 4], ALU.add).then_inc(s[f"level{w}"], 1)

            def gap_square(p, w):
                dve.wait_ge(s[f"level{w}"], p + 1)
                dve.scalar_tensor_tensor(gap_sq[w][:, :], gap[w][:, :], D / 4.0, gap[w][:, :], ALU.mult, ALU.mult)\
                   .then_inc(s[f"gap_sq{w}"], 1)

            def variance(p, w):
                dve.wait_ge(s[f"gap_sq{w}"], p + 1)
                dve.tensor_tensor(dvar[w][:, :], gap_sq[w][:, :], spread[w][:, :], ALU.add).then_inc(s[f"dvar{w}"], 1)

            def inverse(p, w):
                dve.wait_ge(s[f"sd{w}"], p + 1)
                dve.reciprocal(rs[w][:, :], sd[w][:, :]).then_inc(s[f"rs{w}"], 1)

            def shift(p):
                dve.wait_ge(s["rsA"], p + 1)
                dve.scalar_tensor_tensor(shiftA[:, :], mean2["A"][:, :], -0.5, rs["A"][:, :], ALU.mult, ALU.mult)\
                   .then_inc(s["shiftA"], 1)

            def low_rows(p, q):
                dve.wait_ge(s["row_high"], p + 1)
                for g in range(2):
                    part = slice(g * T, (g + 1) * T)
                    dve.tensor_tensor(row16[q][:, part, D:2 * D], row32[:, part, :], row16[q][:, part, 0:D], ALU.subtract)\
                       .then_inc(s["row_low"], 1)
                dve.tensor_copy(row[q][:, :, :, D:RW].bitcast(i32).rearrange("p k t a -> p k (t a)"),
                                result_rows[:, at(p), :, :].rearrange("p o k t -> p (o k) t"))

            def degree_floor(p):
                dve.wait_ge(s["sum_ps"], p + 1)
                dve.tensor_scalar(degm[:, :], ps_deg[:, :], 1.0, None, ALU.max).then_inc(s["degm"], 1)

            def degree_inverse(p):
                dve.wait_ge(s["degm"], p + 1)
                dve.reciprocal(degr[:, :], degm[:, :]).then_inc(s["degr"], 1)

            def degree_weight(p):
                dve.wait_ge(s["degr"], p + 1)
                dve.scalar_tensor_tensor(degw[:, :], ps_deg[:, :], 0.0, degr[:, :], ALU.is_gt, ALU.mult).then_inc(s["degw"], 1)

            def hidden_bias(e):
                to = h_bias[:, bass.ds(e * C, C)]
                dve.tensor_tensor(to, ps_hb[:, :], b1T[:, bass.ds(e * C, C)], ALU.add).then_inc(s["h_bias"], 1)

            def add_messages(p, q):
                dve.wait_ge(s["degw"], p + 1)
                dve.wait_ge(s["upd"], 2 * p + 2)
                for t in range(Q):
                    last = dve.scalar_tensor_tensor(summed[:, t, :], ps_sum[t // T][:, (t % T) * D:(t % T + 1) * D], degw[:, t:t + 1],
                                                    upd[q][:, t, :], ALU.mult, ALU.add)
                last.then_inc(s["summed"], 1)

            def residual(p):
                dve.wait_ge(s["summed"], p + 1)
                for g in range(2):
                    dve.scalar_tensor_tensor(pair_x2(p, g), summed[:, g * T:(g + 1) * T, :], 0.0, pair_x2(p, g), ALU.max, ALU.add)\
                       .then_inc(s["x2"], 1)

            def biased_logits_a(p, q):
                dve.wait_ge(s["logit_ps"], p + 1)
                dve.tensor_tensor(lg0[:, :, :], ps_logit[:, :].rearrange("p (t e) -> p t e", t=Q), wide(sd2[q][:, :]), ALU.mult)\
                   .then_inc(s["lg0"], 1)

            def biased_logits_b(p):
                dve.wait_ge(s["lg0"], p + 1)
                dve.tensor_tensor(lg[:, :, :], lg0[:, :, :], br_all[:, :].unsqueeze(1).to_broadcast([P, Q, E]), ALU.add)\
                   .then_inc(s["lg"], 1)

            def largest(p, k):
                logits, ready = ((lg, "lg"), (lg2, "lg2"))[k]
                dve.wait_ge(s[ready], p + 1)
                dve.tensor_reduce(top[:, k, :], logits[:, :, :], AX, ALU.max).then_inc(s[f"top{k + 1}"], 1)

            def hits(p, k):
                dve.wait_ge(s[f"top{k + 1}"], p + 1)
                dve.tensor_tensor(hit[k][:, :, :], (lg, lg2)[k][:, :, :], wide(top[:, k, :]), ALU.is_equal).then_inc(s[f"hit{k + 1}"], 1)

            def keys(p, k):
                dve.wait_ge(s[f"hit{k + 1}"], p + 1)
                dve.scalar_tensor_tensor(key[k][:, :, :], hit[k][:, :, :], -float(E), expert_no8[:, :, :], ALU.mult, ALU.add)\
                   .then_inc(s[f"key{k + 1}"], 1)

            def choose(p, k):
                dve.wait_ge(s[f"key{k + 1}"], p + 1)
                dve.tensor_reduce(chosen[k][:, :], key[k][:, :, :], AX, ALU.min).then_inc(s[f"chosen{k + 1}"], 1)

            def mark(p, k):
                dve.wait_ge(s[f"chosen{k + 1}"], p + 1)
                dve.tensor_tensor(onehot[:, k, :, :], expert_no[:, :, :], wide(chosen[k][:, :]), ALU.is_equal)\
                   .then_inc(s[f"onehot{k + 1}"], 1)

            def without_first(p):
                dve.wait_ge(s["onehot1"], p + 1)
                dve.scalar_tensor_tensor(lg2[:, :, :], onehot[:, 0, :, :], -FAR, lg[:, :, :], ALU.mult, ALU.add)\
                   .then_inc(s["lg2"], 1)

            def members(p):
                dve.tensor_tensor(margin[:, at(p), :].rearrange("p o t -> p (o t)"), top[:, 1, :], top[:, 0, :], ALU.subtract)
                dve.wait_ge(s["onehot2"], p + 1)
                dve.tensor_tensor(member[:, :, :], onehot[:, 0, :, :], onehot[:, 1, :, :], ALU.add).then_inc(s["member"], 1)

            def low_messages(p, g, q):
                part = slice(g * T, (g + 1) * T)
                dve.wait_ge(s["msg_high"], 2 * p + g + 1)
                dve.tensor_tensor(msgl[q][:, part, :], ps_msg[g][:, :].rearrange("p (t d) -> p t d", t=T), msgh[q][:, part, :],
                                  ALU.subtract).then_inc(s["msg_low"], 1)

            def inner_a(p):
                dve.wait_ge(s["rsB"], p + 1)
                dve.tensor_tensor(half_out[:, :], dvar["B"][:, :], rs["B"][:, :], ALU.mult).then_inc(s["half_out"], 1)

            def inner_b(p):
                dve.wait_ge(s["half_out"], p + 1)
                dve.tensor_tensor(dvar2[:, :], half_out[:, :], rs["B"][:, :], ALU.mult).then_inc(s["dvar2"], 1)

            def places(p):
                dve.wait_ge(s["rank_ps"], p + 1)
                dve.tensor_tensor(pos[:, :, :], ps_rank[:, :].rearrange("p (t e) -> p t e", t=Q),
                                  free_row[:, :].unsqueeze(1).to_broadcast([P, Q, E]), ALU.add).then_inc(s["pos"], 1)

            def pick(p):
                dve.wait_ge(s["pos"], p + 1)
                dve.tensor_tensor(free_row[:, :], free_row[:, :], ps_placed[:, :], ALU.add).then_inc(s["free_row"], 1)
                dve.tensor_tensor(picked[:, :, :, :], onehot[:, :, :, :],
                                  pos[:, :, :].unsqueeze(1).to_broadcast([P, K, Q, E]), ALU.mult).then_inc(s["picked"], 1)

            def destinations(p, q):
                dve.wait_ge(s["picked"], p + 1)
                with nc.allow_low_precision(reason="summed in float32: one whole number under 2 ** 24, and zeros"):
                    dve.tensor_reduce(dest[q][:, :, :], picked[:, :, :, :], AX, ALU.add).then_inc(s["dest"], 1)

            def rows_a(p, q):
                dve.wait_ge(s["sd2"], p + 1)
                dve.reciprocal(rs2[:, :], sd2[q][:, :]).then_inc(s["rs2"], 1)
                dve.tensor_scalar(meanB[:, :], mean2["B"][:, :], 0.5, None, ALU.mult)

            def rows_b(p):
                dve.wait_ge(s["rs2"], p + 1)
                dve.tensor_tensor(rsBoth[:, :], rs["B"][:, :], rs2[:, :], ALU.mult).then_inc(s["rsBoth"], 1)

            def rows_c(p):
                dve.wait_ge(s["rsBoth"], p + 1)
                for t in range(Q):
                    last = dve.tensor_scalar(row32[:, t, :], block_x2(p, t), meanB[:, t:t + 1], rsBoth[:, t:t + 1],
                                             ALU.subtract, ALU.mult)
                last.then_inc(s["row32"], 1)

            def low_weights(e, q):
                dve.wait_ge(s["w1h"], e + 1)
                dve.scalar_tensor_tensor(W1l[:, part_of(e)], W1_in[q][:, :], gain[:, at(e)], W1h[:, part_of(e)],
                                         ALU.mult, ALU.subtract).then_inc(s["w1l"], 1)
                dve.wait_ge(s["w2h"], e + 1)
                dve.scalar_tensor_tensor(W2l[:, part_of(e)], W2_in[q][:, :, :].rearrange("p c d -> p (c d)"), WSCALE, W2h[:, part_of(e)],
                                         ALU.mult, ALU.subtract).then_inc(s["w2l"], 1)

            def step(n, q):
                ahead, first, second, third = has(n, 0), has(n, 1), has(n, 2), has(n, 3)
                if first:
                    inverse(n - 1, "A")
                if second:
                    degree_floor(n - 2)
                    hidden_bias(n - 2)
                if first:
                    shift(n - 1)
                if second:
                    degree_inverse(n - 2)
                if third:
                    low_rows(n - 3, 1 - q)
                if second:
                    degree_weight(n - 2)
                    add_messages(n - 2, q)
                    residual(n - 2)
                if third:
                    biased_logits_a(n - 3, 1 - q)
                if second:
                    block_stats(n - 2, "B", q, (0, 1))
                if third:
                    biased_logits_b(n - 3)
                if second:
                    block_stats(n - 2, "B", q, (2, 3))
                if third:
                    largest(n - 3, 0)
                if second:
                    block_stats(n - 2, "B", q, (4, 5))
                if third:
                    hits(n - 3, 0)
                if second:
                    block_stats(n - 2, "B", q, (6, 7))
                if third:
                    keys(n - 3, 0)
                if second:
                    both_halves(n - 2, "B", 4 * (n - 2) + 4)
                if third:
                    choose(n - 3, 0)
                if second:
                    gap_square(n - 2, "B")
                if third:
                    mark(n - 3, 0)
                if second:
                    variance(n - 2, "B")
                if third:
                    without_first(n - 3)
                if first:
                    low_messages(n - 1, 0, 1 - q)
                if third:
                    largest(n - 3, 1)
                if first:
                    low_messages(n - 1, 1, 1 - q)
                if third:
                    hits(n - 3, 1)
                if second:
                    inverse(n - 2, "B")
                if third:
                    keys(n - 3, 1)
                if second:
                    inner_a(n - 2)
                if third:
                    choose(n - 3, 1)
                if second:
                    inner_b(n - 2)
                if third:
                    mark(n - 3, 1)
                if ahead:
                    block_stats(n, "A", q, (0, 1, 2, 3))
                if third:
                    members(n - 3)
                if ahead:
                    block_stats(n, "A", q, (4, 5, 6, 7))
                if second:
                    rows_a(n - 2, q)
                if ahead:
                    both_halves(n, "A", 2 * n + 2)
                if second:
                    rows_b(n - 2)
                if ahead:
                    gap_square(n, "A")
                if third:
                    places(n - 3)
                if ahead:
                    variance(n, "A")
                if third:
                    pick(n - 3)
                if second:
                    rows_c(n - 2)
                if third:
                    destinations(n - 3, 1 - q)
                if first:
                    low_weights(n - 1, 1 - q)

            pair_steps(dve, step)

            dve.wait_ge(s["free_row"], H)
            dve.tensor_copy(free_int[:, :], free_row[0:1, :]).then_inc(s["free_int"], 1)
            dve.scalar_tensor_tensor(count[:, :], expert_no[0:1, 0, :], -float(REGION), free_row[0:1, :], ALU.mult, ALU.add)\
               .then_inc(s["cnt"], 1)
            dve.wait_ge(s["cnt"], 1)
            dve.tensor_tensor(over[:, :, :], count[:, :].unsqueeze(2).to_broadcast([1, E, NODES // ROWS]), steps32[:, :, :], ALU.is_gt)\
               .then_inc(s["over"], 1)
            dve.wait_ge(s["over"], 1)
            dve.tensor_reduce(ntile[:, :], over[:, :, :], AX, ALU.add).then_inc(s["ntile"], 1)
            dve.wait_ge(s["ntile"], 1)
            dve.tensor_tensor(prod[:, :, :], ntile[:, :].unsqueeze(1).to_broadcast([1, E, E]), upto[:, :, :], ALU.mult)\
               .then_inc(s["prod"], 1)
            dve.tensor_scalar(jump[:, :], ntile[:, :], -float(ROWS), float(REGION), ALU.mult, ALU.add).then_inc(s["jump"], 1)
            dve.wait_ge(s["prod"], 1)
            dve.tensor_reduce(tile_end[:, :], prod[:, :, :], AX, ALU.add).then_inc(s["tile_end"], 1)
            dve.wait_ge(s["tile_end"], 1)
            dve.tensor_tensor(past[:, :, :], tile_no[:, :, :], tile_end[:, :].unsqueeze(1).to_broadcast([1, TILES, E]), ALU.is_ge)\
               .then_inc(s["past"], 1)
            dve.wait_ge(s["past"], 1)
            dve.wait_ge(s["jump"], 1)
            dve.tensor_reduce(t_expert[:, :], past[:, :, :], AX, ALU.add).then_inc(s["t_expert"], 1)
            dve.tensor_tensor(moved[:, :, :], past[:, :, :], jump[:, :].unsqueeze(1).to_broadcast([1, TILES, E]), ALU.mult)\
               .then_inc(s["moved"], 1)
            dve.wait_ge(s["moved"], 1)
            dve.tensor_reduce(t_row[:, :], moved[:, :, :], AX, ALU.add).then_inc(s["t_row0"], 1)
            dve.wait_ge(s["t_row0"], 1)
            dve.scalar_tensor_tensor(t_row[:, :], tile_no[:, :, 0], float(ROWS), t_row[:, :], ALU.mult, ALU.add)\
               .then_inc(s["t_row1"], 1)
            dve.wait_ge(s["t_row1"], 1)
            dve.tensor_scalar(tile_expert[:, :], t_expert[:, :], float(E - 1), None, ALU.min)
            dve.tensor_scalar(tile_row[:, :], t_row[:, :], float(SPARE), None, ALU.min).then_inc(s["table"], 1)

            dve.wait_ge(s["ex"], 1)
            dve.tensor_scalar(ex1[:, :], ex[:, :], 1.0, None, ALU.add).then_inc(s["ex1"], 1)
            dve.wait_ge(s["ex1"], 1)
            dve.reciprocal(weight[:, 0, :], ex1[:, :]).then_inc(s["wt0"], 1)
            dve.wait_ge(s["wt0"], 1)
            dve.tensor_tensor(weight[:, 1, :], weight[:, 0, :], ex[:, :], ALU.mult).then_inc(s["weight"], 1)

            def note(t, q):
                loaded(dve, "tin", t, q)
                dve.tensor_copy(result_row[:, at(t), :].rearrange("p o u -> p (o u)"),
                                tin[q][:, :, D:RW].bitcast(u32).rearrange("p u a -> p (u a)")).then_inc(s["result_row"], 1)

            def split(t, q):
                for half in range(2):
                    part = slice(half * (C // 2), (half + 1) * (C // 2))
                    dve.wait_ge(s["gel"], 2 * t + half + 1)
                    dve.tensor_copy(gelh[q][:, part, :], gel[q][:, part, :]).then_inc(s["gelh"], 1)
                    dve.wait_ge(s["gelh"], 2 * t + half + 1)
                    dve.tensor_tensor(gell[q][:, part, :], gel[q][:, part, :], gelh[q][:, part, :], ALU.subtract)\
                       .then_inc(s["gell"], 1)

            def finish(t, q):
                e = dve.value_load(tile_expert[0:1, at(t)], min_val=0, max_val=E - 1)
                dve.wait_ge(s["y_ps"], t + 1)
                if later(t, 2):
                    dve.wait_ge(s[f"sent{q}"], 16 * SUB * (t // 2) if isinstance(t, int) else 8 * SUB * (t - q))
                dve.tensor_copy(send_to[q][:, :], result_row[:, at(t), :].rearrange("p o u -> p (o u)"))
                dve.scalar_tensor_tensor(y[q][:, :, :], ps_y[q][:, 0:SUB * D].rearrange("p (u d) -> p u d", u=SUB), 1.0 / WSCALE,
                                         b2_all[:, bass.ds(e, 1), :].to_broadcast([P, SUB, D]), ALU.mult, ALU.add)\
                   .then_inc(s["y"], 1)

            def tile_step(n, q):
                if has(n, 2, TILES):
                    finish(n - 2, q)
                if has(n, -1, TILES):
                    note(n + 1, 1 - q)
                if has(n, 0, TILES):
                    split(n, q)

            dve.wait_ge(s["gains_in"], 16)
            note(0, 0)
            tile_steps(dve, tile_step)

            x2_blocks = x2[:, :, :, :].rearrange("p h t d -> p (h t) d")

            def combine(b, q):
                loaded(dve, "yk", b, q, 16 * K)
                dve.wait_ge(s["weight"], 1)
                if later(b, 1):
                    dve.wait_ge(s["total"], b)
                for t in range(T):
                    last = dve.scalar_tensor_tensor(first[:, t, :], yk[q][:, 0, t, :], weight[:, 0, at(b * T + t)], x2_blocks[:, at(b * T + t), :].rearrange("p o d -> p (o d)"),
                                                    ALU.mult, ALU.add)
                last.then_inc(s["first"], 1)
                dve.wait_ge(s["first"], b + 1)
                dve.wait_ge(s["second"], b + 1)
                if later(b, 2):
                    dve.wait_ge(s[f"stored{q}"], 16 * (b // 2) if isinstance(b, int) else 8 * (b - q))
                dve.tensor_tensor(total[q][:, :, :], first[:, :, :], second[q][:, :, :], ALU.add).then_inc(s["total"], 1)

            combine(0, 0)
            combine(1, 1)
            with dve.Fori(2, B - 1, 2) as b:
                combine(b, 0)
                combine(b + 1, 1)


_INS = ["x", "adj", "L0_gnn_W_msg", "L0_gnn_W_upd", "L0_gnn_bias", "L0_ffn_Wr", "L0_ffn_br", "L0_ffn_ln_g", "L0_ffn_ln_b",
        "L0_ffn_W1", "L0_ffn_b1", "L0_ffn_W2", "L0_ffn_b2"]


def kernel(**inputs):
    import numpy as _np
    import concourse.bacc as _bacc
    from concourse import mybir as _mybir
    from concourse.bass_utils import run_bass_kernel_spmd as _run

    nc = _bacc.Bacc("TRN2", target_bir_lowering=False, num_devices=1)
    arrays, args = {}, []
    for name in _INS:
        a = _np.ascontiguousarray(inputs[name])
        arrays[f"in_{name}_dram"] = a
        args.append(nc.dram_tensor(f"in_{name}_dram", a.shape, _mybir.dt.from_np(a.dtype), kind="ExternalInput").ap())
    args.append(nc.dram_tensor("out_dram", (16, 512, 128), _mybir.dt.float32, kind="ExternalOutput").ap())
    graph_then_experts_kernel(nc, *args)
    r = _run(nc, [arrays], core_ids=[0])
    return r.results[0]["out_dram"]
```

```python
import concourse.bass as bass
from concourse import mybir
from contextlib import ExitStack


def graph_then_experts_kernel(nc, x, adj, W_msg, W_upd, bias, Wr, br, ln_g, ln_b, W1, b1, W2, b2, out):
    fp32, fp16, i32, u32 = mybir.dt.float32, mybir.dt.float16, mybir.dt.int32, mybir.dt.uint32
    ALU = mybir.AluOpType
    ACT = mybir.ActivationFunctionType
    AX = mybir.AxisListType.X

    P = 128
    B, N, D = x.shape
    E, _, HID = W1.shape
    K = 2
    T = N // P
    C = HID // P
    NODES = B * N
    H = B // 2
    Q = 2 * T
    ROWS = 512
    SUB = ROWS // P
    REGION = NODES + ROWS
    TILES = K * NODES // ROWS + E - 1
    SPARE = E * REGION
    RW = D + 1
    FULL = K * NODES // (E * ROWS)
    EARLY = FULL + 1
    NOWHERE = 1 << 20
    EPS = 1e-5
    WSCALE = 64.0
    FAR = 3e38

    rows = nc.dram_tensor("expert_rows", [SPARE + ROWS, RW], fp32, kind="Internal").ap()
    results = nc.dram_tensor("expert_results", [K * NODES, D], fp32, kind="Internal").ap()

    ctx = ExitStack()
    with ctx:
        def sb(name, shape, dt=fp32):
            return ctx.enter_context(nc.sbuf_tensor(name, shape, dt))

        def pb(name, shape, dt=fp32):
            return ctx.enter_context(nc.psum_tensor(name, shape, dt))

        def sem(name):
            return ctx.enter_context(nc.semaphore(name))

        ident = sb("ident", [P, P])
        ident16 = sb("ident16", [P, P], fp16)
        earlier = sb("earlier", [P, P], fp16)
        ones16 = sb("ones16", [P, P], fp16)
        held = sb("held", [P, 1], fp16)
        eps_col = sb("eps_col", [P, 1])
        warm = sb("warm", [P, 1])
        expert_no = sb("expert_no", [P, Q, E])
        expert_no8 = sb("expert_no8", [P, Q, E])
        result_rows = sb("result_rows", [P, H, K, Q], i32)
        br_all = sb("br_all", [P, E])
        bias_row = sb("bias_row", [1, D])
        bias_h = sb("bias_h", [1, D], fp16)
        bias_l = sb("bias_l", [1, D], fp16)
        b2_all = sb("b2_all", [P, E, D])
        pad_rows = sb("pad_rows", [P, SUB, RW])
        Wm_sb = sb("Wm_sb", [D, D])
        Wu_sb = sb("Wu_sb", [D, D])
        Wr_sb = sb("Wr_sb", [D, E])
        Wrh = sb("Wrh", [D, E], fp16)
        Wrl = sb("Wrl", [D, E], fp16)

        W1h = sb("W1h", [D, E * HID], fp16)
        W1l = sb("W1l", [D, E * HID], fp16)
        W2h = sb("W2h", [P, E * C * D], fp16)
        W2l = sb("W2l", [P, E * C * D], fp16)
        gb_rows = sb("gb_rows", [2 * E, D])
        b1_rows = sb("b1_rows", [E * C, P])
        gain = sb("gain", [D, E])
        offset = sb("offset", [D, E])
        b1T = sb("b1T", [P, E * C])
        h_bias = sb("h_bias", [P, E * C])

        x2 = sb("x2", [P, H, Q, D])
        adj_int = [sb(f"adj_int{g}", [P, T, N], i32) for g in range(2)]
        adj16 = [[sb(f"adj16_{q}{g}", [P, T, N], fp16) for g in range(2)] for q in range(2)]
        xn = sb("xn", [P, Q, D])
        xnT = sb("xnT", [D, 2 * N])
        msgh = [sb(f"msgh{q}", [P, Q, D], fp16) for q in range(2)]
        msgl = [sb(f"msgl{q}", [P, Q, D], fp16) for q in range(2)]
        upd = [sb(f"upd{q}", [P, Q, D]) for q in range(2)]
        summed = sb("summed", [P, Q, D])
        row32 = sb("row32", [P, Q, D])
        row = [sb(f"row{q}", [P, K, Q, RW]) for q in range(2)]
        parts = sb("parts", [P, Q, 2 * D], fp16)
        rowT = sb("rowT", [D, 2, 2 * N], fp16)
        member = sb("member", [P, Q, E], fp16)
        dest = [sb(f"dest{q}", [P, K, Q], u32) for q in range(2)]
        stats = {w: sb(f"stats{w}", [P, Q, 6]) for w in "AB"}
        mean2 = {w: sb(f"mean2{w}", [P, Q]) for w in "AB"}
        gap = {w: sb(f"gap{w}", [P, Q]) for w in "AB"}
        spread = {w: sb(f"spread{w}", [P, Q]) for w in "AB"}
        gap_sq = {w: sb(f"gap_sq{w}", [P, Q]) for w in "AB"}
        dvar = {w: sb(f"dvar{w}", [P, Q]) for w in "AB"}
        sd = {w: sb(f"sd{w}", [P, Q]) for w in "AB"}
        rs = {w: sb(f"rs{w}", [P, Q]) for w in "AB"}
        shiftA = sb("shiftA", [P, Q])
        half_out = sb("half_out", [P, Q])
        dvar2 = sb("dvar2", [P, Q])
        sd2 = [sb(f"sd2{q}", [P, Q]) for q in range(2)]
        rs2 = sb("rs2", [P, Q])
        rsBoth = sb("rsBoth", [P, Q])
        meanB = sb("meanB", [P, Q])
        degm = sb("degm", [P, Q])
        degr = sb("degr", [P, Q])
        degw = sb("degw", [P, Q])
        lg0 = sb("lg0", [P, Q, E])
        lg = sb("lg", [P, Q, E])
        lg2 = sb("lg2", [P, Q, E])
        top = sb("top", [P, K, Q])
        hit = [sb(f"hit{k}", [P, Q, E]) for k in range(K)]
        key = [sb(f"key{k}", [P, Q, E]) for k in range(K)]
        chosen = [sb(f"chosen{k}", [P, Q]) for k in range(K)]
        onehot = sb("onehot", [P, K, Q, E])
        pos = sb("pos", [P, Q, E])
        picked = sb("picked", [P, K, Q, E])
        free_row = sb("free_row", [P, E])
        margin = sb("margin", [P, H, Q])

        free_int = sb("free_int", [1, E], i32)
        count = sb("count", [1, E])
        steps32 = sb("steps32", [1, E, NODES // ROWS])
        over = sb("over", [1, E, NODES // ROWS])
        ntile = sb("ntile", [1, E])
        upto = sb("upto", [1, E, E])
        prod = sb("prod", [1, E, E])
        tile_end = sb("tile_end", [1, E])
        jump = sb("jump", [1, E])
        tile_no = sb("tile_no", [1, TILES, E])
        past = sb("past", [1, TILES, E])
        moved = sb("moved", [1, TILES, E])
        t_expert = sb("t_expert", [1, TILES])
        t_row = sb("t_row", [1, TILES])
        tile_expert = sb("tile_expert", [1, TILES], i32)
        tile_row = sb("tile_row", [1, TILES], i32)

        before = sb("before", [1, H, E])
        own = sb("own", [1, EARLY, E])
        limit = sb("limit", [1, EARLY])
        short = sb("short", [1, EARLY, H - 1, E])
        own_short = sb("own_short", [1, EARLY, H - 1, E])
        more = sb("more", [1, EARLY, H - 1])
        needed = sb("needed", [1, 2, EARLY])
        pads_part = sb("pads_part", [1, EARLY])
        needed_pads = sb("needed_pads", [1, EARLY], i32)
        needed_rows = sb("needed_rows", [1, 2, EARLY], i32)

        W1_raw = [adj_int[i][:, :, :].bitcast(fp32) for i in range(2)]
        W2_raw = [adj16[i // 2][i % 2][:, :, :].rearrange("p t n -> p (t n)").bitcast(fp32).rearrange("p (a d) -> p a d", d=D)
                  for i in range(4)]

        tin = [sb(f"tin{q}", [P, SUB, RW]) for q in range(2)]
        result_row = sb("result_row", [P, TILES, SUB], u32)
        tin16 = [tin[q][:, :, :].bitcast(fp16) for q in range(2)]
        tT = [sb(f"tT{q}", [D, 2, ROWS], fp16) for q in range(2)]
        gel = [adj_int[q][:, :, :].bitcast(fp32) for q in range(2)]
        gelh, gell = [adj16[q][0] for q in range(2)], [adj16[q][1] for q in range(2)]
        y = [sb(f"y{q}", [P, SUB, D]) for q in range(2)]
        send_to = [sb(f"send_to{q}", [P, SUB], u32) for q in range(2)]

        weight = sb("weight", [P, K, B * T])
        ex = sb("ex", [P, B * T])
        ex1 = sb("ex1", [P, B * T])
        yk = [w[:, :].bitcast(fp32).rearrange("p (k t d) -> p k t d", k=K, t=Q) for w in (W1h, W1l, W2h, W2l)]
        second = [gel[q][:, 0:2, :].rearrange("p a (t d) -> p (a t) d", t=T) for q in range(2)]
        total = [adj16[i // 2][i % 2][:, :, :].rearrange("p t n -> p (t n)").bitcast(fp32).rearrange("p (t d) -> p t d", t=Q)
                 for i in range(4)]
        first = [xn, summed]

        bank = [pb(f"bank{i}", [P, 512]) for i in range(8)]
        ps_sum, ps_msg = bank[0:2], bank[2:4]
        ps_upd, ps_xnT, ps_rowT, ps_small = bank[4:8]
        ps_logit = ps_small[:, 0:Q * E]
        ps_rank = ps_small[:, Q * E:2 * Q * E]
        ps_placed = ps_small[:, 2 * Q * E:2 * Q * E + E]
        ps_deg = ps_small[:, 256:256 + Q]
        ps_gains, ps_hb = ps_upd[:, 0:64], ps_upd[:, 64:64 + E * C]
        ps_h = [bank[c][:, :] for c in range(C)]
        ps_tT = [bank[4 + q][:, :].bitcast(fp16) for q in range(2)]
        ps_y = bank[6:8]

        names = """x_in0 x_in1 adj_in0 adj_in1 msg_w_in const_in gains_in w1_in w2_in
            const_id0 const_id const_id16 wr_high wr_low bias_high bias_low const_tri0 const_tri const_pool
            bnA levelA gap_sqA dvarA sdA rsA shiftA xn xnT_ps xnT msg_ps upd_ps msg_high msg_low upd adj16
            sum_ps degm degr degw summed x2 bnB levelB gap_sqB dvarB sdB rsB half_out dvar2 sd2 rs2 rsBoth row32 row_high row_low
            rowT_ps rowT row_copied0 row_copied1 logit_ps lg0 lg lg2 member rank_ps pos picked dest free_row
            top1 hit1 key1 chosen1 onehot1 top2 hit2 key2 chosen2 onehot2 scattered0 scattered1
            gbT_ps gain offset b1T hb_ps h_bias w1h w1l w2h w2l
            cnt over ntile prod tile_end jump past t_expert moved t_row0 t_row1 table free_int own short own_short more needed needed_rows
            first_pads pads held
            tin0 tin1 tT_ps tT result_row h_ps gel gelh gell y_ps y sent0 sent1
            ex ex1 wt0 weight y0_in0 y0_in1 y0_in2 y0_in3 y1_in0 y1_in1 y1_in2 y1_in3 second first total stored0 stored1 stored2 stored3""".split()
        s = {n: sem(n) for n in names}

        const_loads = [(Wu_sb[:, :], W_upd),
                       (bias_row[:, :], bias.rearrange("(a n) -> a n", a=1)), (Wr_sb[:, :], Wr),
                       (br_all[:, :], br.rearrange("(a n) -> a n", a=1).broadcast_to([P, E]))]
        gain_loads = [(gb_rows[0:E, :], ln_g), (gb_rows[E:2 * E, :], ln_b),
                      (b1_rows[:, :], b1.rearrange("e (c p) -> (e c) p", p=P)),
                      (b2_all[:, :, :], b2.rearrange("(a e) d -> a e d", a=1).broadcast_to([P, E, D]))]

        block = ctx.enter_context(nc.Block())

        def pair_steps(eng, step):
            for n in range(4):
                step(n, n % 2)
            with eng.Fori(4, H - 1, 2) as n:
                step(n, 0)
                step(n + 1, 1)
            for n in (H, H + 1, H + 2):
                step(n, n % 2)

        def tile_steps(eng, step):
            for n in range(4):
                step(n, n % 2)
            with eng.Fori(4, TILES - 2, 2) as n:
                step(n, 0)
                step(n + 1, 1)
            for n in (TILES - 1, TILES, TILES + 1):
                step(n, n % 2)

        def sum_steps(eng, step):
            for i in range(4):
                step(i, i)
            with eng.Fori(4, H - 3, 4) as p:
                for i in range(4):
                    step(p + i, i)

        def results_loaded(eng, k, p, i):
            eng.wait_ge(s[f"y{k}_in{i}"], 16 * (p // 4 + 1) if isinstance(p, int) else (p - i) * 4 + 16)

        def has(n, lag, count=H):
            return not isinstance(n, int) or 0 <= n - lag < count

        def later(n, least):
            return not isinstance(n, int) or n >= least

        def loaded(eng, name, n, q, each=16):
            eng.wait_ge(s[f"{name}{q}"], each * (n // 2 + 1) if isinstance(n, int) else (n - q) * (each // 2) + each)

        def scattered(p, q):
            return 16 * K * Q * (p // 2) if isinstance(p, int) else (p - q - 1) * (8 * K * Q) + 8 * K * Q

        def at(n):
            return slice(n, n + 1) if isinstance(n, int) else bass.ds(n, 1)

        def pair_of(p):
            return slice(2 * p, 2 * p + 2) if isinstance(p, int) else bass.ds(2 * p, 2)

        def pair_x2(p, g=None):
            part = slice(0, Q) if g is None else slice(g * T, (g + 1) * T)
            return x2[:, at(p), part, :].rearrange("p o t d -> p (o t) d")

        def block_x2(p, t):
            return x2[:, at(p), t, :].rearrange("p o d -> p (o d)")

        def region_part(start):
            return rows[bass.ds(start, ROWS), :].rearrange("(p s) w -> p s w", p=P)

        @block.sync
        def _(sp):
            def load_x(n, q):
                sp.dma_start(x2[:, at(n), :, :].rearrange("p o t d -> p (o t) d"),
                             x[pair_of(n)].rearrange("g (t p) d -> p (g t) d", p=P)).then_inc(s[f"x_in{q}"], 16)

            load_x(0, 0)
            load_x(1, 1)

            def load_gains():
                for dst, src in gain_loads:
                    sp.dma_start(dst, src).then_inc(s["gains_in"], 16)
                sp.wait_ge(s["const_pool"], 1)
                sp.dma_start(region_part(SPARE), pad_rows[:, :, :]).then_inc(s["pads"], 16)

            def load_first_weights():
                sp.wait_ge(s["adj16"], B)
                for i in range(2):
                    sp.dma_start(W1_raw[i], W1.rearrange("e d h -> d e h")[:, 4 * i:4 * i + 4, :]).then_inc(s["w1_in"], 16)

            def load_second_weights():
                sp.wait_ge(s["sum_ps"], H)
                for i in range(4):
                    sp.dma_start(W2_raw[i], W2.rearrange("e (c h) d -> h (e c) d", h=P)[:, 2 * C * i:2 * C * (i + 1), :])\
                        .then_inc(s["w2_in"], 16)

            def step(n, q):
                if isinstance(n, int) and n == 3:
                    load_gains()
                if isinstance(n, int) and n == H:
                    load_first_weights()
                if isinstance(n, int) and n == H + 1:
                    load_second_weights()
                if has(n, 0):
                    if later(n, 2):
                        sp.wait_ge(s["dvarA"], n - 1)
                        load_x(n, q)
                    if not later(n, 1):
                        sp.wait_ge(s["const_in"], 16 * len(const_loads))
                    for g in range(2):
                        if later(n, 1):
                            sp.wait_ge(s["adj16"], 2 * n + g - 1)
                        sp.dma_start(adj_int[g][:, :, :], adj[at(2 * n + g)].rearrange("o (t p) n -> p (o t) n", p=P))\
                            .then_inc(s[f"adj_in{g}"], 16)
                if has(n, 3):
                    p, r = n - 3, 1 - q
                    made, through = 2 * p + 2, scattered(p, r)
                    sp.wait_ge(s["row_low"], made)
                    if later(p, 2):
                        sp.wait_ge(s[f"scattered{r}"], through)
                    for k in range(K):
                        sp.dma_start(row[r][:, k, :, 0:D], parts[:, :, :].bitcast(fp32)).then_inc(s[f"row_copied{r}"], 16)

            pair_steps(sp, step)

            sp.wait_ge(s["free_int"], 1)
            start = sp.value_load(free_int[0:1, 0:1], min_val=0, max_val=NODES)
            sp.dma_start(region_part(start), pad_rows[:, :, :]).then_inc(s["first_pads"], 16)

            sp.wait_ge(s["table"], 1)
            sp.wait_ge(s["needed_rows"], 1)

            def load_tile(t, q, counts=()):
                start = sp.value_load(tile_row[0:1, at(t)], min_val=0, max_val=SPARE)
                if counts:
                    sp.wait_ge(s["first_pads"], 16)
                for name, count in zip(("scattered0", "scattered1", "pads"), counts):
                    sp.wait_ge(s[name], count)
                if later(t, 2):
                    sp.wait_ge(s["tT_ps"], t - 1)
                    sp.wait_ge(s["result_row"], t - 1)
                sp.dma_start(tin[q][:, :, :], region_part(start)).then_inc(s[f"tin{q}"], 16)

            for t in range(EARLY):
                most = 16 * K * Q * (H // 2)
                counts = [sp.value_load(needed_rows[0:1, q, t:t + 1], min_val=16 * K * Q, max_val=most) for q in range(2)]
                counts.append(sp.value_load(needed_pads[0:1, t:t + 1], min_val=16, max_val=16 * E))
                load_tile(t, t % 2, counts)
            sp.wait_ge(s["pads"], 16 * E)
            for q in range(2):
                sp.wait_ge(s[f"scattered{q}"], most)
            load_tile(EARLY, EARLY % 2)
            with sp.Fori(EARLY + 1, TILES - 2, 2) as t:
                load_tile(t, 0)
                load_tile(t + 1, 1)
            load_tile(TILES - 1, 0)

            for q in range(2):
                sp.wait_ge(s[f"sent{q}"], 16 * SUB * ((TILES + 1 - q) // 2))
            by_pair = results.rearrange("(k h p t) d -> h k p t d", k=K, h=H, p=P)

            def load_results(p, i):
                if later(p, 4):
                    sp.wait_ge(s["first"], p - 3)
                    sp.wait_ge(s["second"], p - 3)
                for k in range(K):
                    sp.dma_start(yk[i][:, k], by_pair[at(p), k].rearrange("o p t d -> p (o t) d")).then_inc(s[f"y{k}_in{i}"], 16)

            sum_steps(sp, load_results)

        @block.gpsimd
        def _(pool):
            pool.memset(ident[:, :], 0.0).then_inc(s["const_id0"], 1)
            pool.wait_ge(s["const_id0"], 1)
            pool.affine_select(out=ident[:, :], in_=ident[:, :], compare_op=ALU.not_equal, fill=1.0,
                               base=0, pattern=[[-1, P]], channel_multiplier=1).then_inc(s["const_id"], 1)
            pool.wait_ge(s["const_id"], 1)
            pool.tensor_copy(ident16[:, :], ident[:, :]).then_inc(s["const_id16"], 1)
            pool.memset(earlier[:, :], 0.0).then_inc(s["const_tri0"], 1)
            pool.wait_ge(s["const_tri0"], 1)
            pool.affine_select(out=earlier[:, :], in_=earlier[:, :], compare_op=ALU.is_ge, fill=1.0,
                               base=0, pattern=[[-1, P]], channel_multiplier=1).then_inc(s["const_tri"], 1)
            pool.memset(ones16[:, :], 1.0)
            pool.memset(upto[:, :, :], 0.0).then_inc(s["const_tri0"], 1)
            pool.wait_ge(s["const_tri0"], 2)
            pool.affine_select(out=upto[:, :, :], in_=upto[:, :, :], compare_op=ALU.is_gt, fill=1.0,
                               base=0, pattern=[[-1, E], [1, E]], channel_multiplier=0)
            pool.iota(expert_no[:, :, :], pattern=[[0, Q], [1, E]], base=0, channel_multiplier=0,
                      allow_small_or_imprecise_dtypes=True)
            pool.iota(expert_no8[:, :, :], pattern=[[0, Q], [1, E]], base=E, channel_multiplier=0,
                      allow_small_or_imprecise_dtypes=True)
            pool.iota(result_rows[:, :, :, :], pattern=[[2 * N, H], [NODES, K], [1, Q]], base=0, channel_multiplier=Q)
            pool.iota(free_row[:, :], pattern=[[REGION, E]], base=0, channel_multiplier=0,
                      allow_small_or_imprecise_dtypes=True)
            pool.iota(steps32[:, :, :], pattern=[[0, E], [ROWS, NODES // ROWS]], base=0, channel_multiplier=0,
                      allow_small_or_imprecise_dtypes=True)
            for slot, tile, count in ((0, 0, FULL - 1), (FULL - 1, FULL + 1, 2), (FULL + 1, FULL - 1, 2),
                                      (FULL + 3, FULL + 3, TILES - FULL - 3)):
                pool.iota(tile_no[:, slot:slot + count, :], pattern=[[1, count], [0, E]], base=tile, channel_multiplier=0,
                          allow_small_or_imprecise_dtypes=True)
            pool.memset(pad_rows[:, :, 0:D], 0.0)
            pool.memset(pad_rows[:, :, D:RW].bitcast(i32), NOWHERE)
            pool.memset(eps_col[:, :], EPS).then_inc(s["const_pool"], 1)

            def hold(before):
                if later(before, 1):
                    pool.wait_ge(s["held"], before)
                pool.tensor_tensor(held[:, :], ones16[:, 0:1], ones16[:, 0:1], ALU.mult).then_inc(s["held"], 1)

            def scatter(n, q):
                if not has(n, 3):
                    return
                p, q = n - 3, 1 - q
                pool.wait_ge(s["dest"], p + 1)
                loaded(pool, "row_copied", p, q, 16 * K)
                hold(p)
                for k in range(K):
                    for t in range(Q):
                        pool.indirect_dma_start(rows, bass.IndirectOffsetOnAxis(ap=dest[q][:, k, t:t + 1], axis=0),
                                                row[q][:, k, t, :], None).then_inc(s[f"scattered{q}"], 16)

            pair_steps(pool, scatter)

            def send(t, q):
                pool.wait_ge(s["y"], t + 1)
                hold(t + H)
                for u in range(SUB):
                    idx = send_to[q][:, u:u + 1]
                    pool.indirect_dma_start(results, bass.IndirectOffsetOnAxis(ap=idx, axis=0), y[q][:, u, :], None,
                                            bounds_check=K * NODES - 1, oob_is_err=False).then_inc(s[f"sent{q}"], 16)

            with pool.Fori(0, TILES - 2, 2) as t:
                send(t, 0)
                send(t + 1, 1)
            send(TILES - 1, 0)

        @block.tensor
        def _(pe):
            pe.wait_ge(s["const_id"], 1)
            pe.wait_ge(s["const_tri"], 1)
            pe.wait_ge(s["const_pool"], 1)
            pe.wait_ge(s["const_id16"], 1)
            def turn_rows(p, g):
                pe.wait_ge(s["row_low"], 2 * p + g + 1)
                if g or later(p, 1):
                    pe.wait_ge(s["rowT"], 2 * p + g)
                to = ps_rowT[:, :].bitcast(fp16)
                for part in range(2):
                    for t in range(T):
                        a = part * N + t * P
                        last = pe.transpose(to[:, a:a + P], parts[:, g * T + t, part * D:(part + 1) * D], ident16[:, :])
                last.then_inc(s["rowT_ps"], 1)

            def turn_nodes(p, g):
                pe.wait_ge(s["xn"], 2 * p + g + 1)
                if g or later(p, 1):
                    pe.wait_ge(s["xnT"], 2 * p + g)
                for t in range(T):
                    last = pe.transpose(ps_xnT[:, t * P:(t + 1) * P], xn[:, g * T + t, :], ident[:, :])
                last.then_inc(s["xnT_ps"], 1)

            def logits(p):
                pe.wait_ge(s["rowT"], 2 * p + 2)
                for t in range(Q):
                    to = ps_logit[:, t * E:(t + 1) * E]
                    high, low = (rowT[:, part, t * P:(t + 1) * P] for part in range(2))
                    pe.matmul(to, high, Wrh[:, :], start=True, stop=False)
                    pe.matmul(to, high, Wrl[:, :], start=False, stop=False)
                    last = pe.matmul(to, low, Wrh[:, :], start=False, stop=True)
                last.then_inc(s["logit_ps"], 1)

            def messages(p, g):
                if isinstance(p, int) and p == 0 and g == 0:
                    for name, count in (("msg_w_in", 16), ("const_in", 16 * len(const_loads)), ("wr_low", 1), ("bias_low", 1)):
                        pe.wait_ge(s[name], count)
                pe.wait_ge(s["xnT"], 2 * p + g + 1)
                if later(p, 1):
                    pe.wait_ge(s["msg_low"], 2 * p + g - 1)
                for t in range(T):
                    a = g * N + t * P
                    last = pe.matmul(ps_msg[g][:, t * D:(t + 1) * D], xnT[:, a:a + P], Wm_sb[:, :], start=True, stop=True)
                last.then_inc(s["msg_ps"], 1)

            def updates(p, g):
                if g or later(p, 1):
                    pe.wait_ge(s["upd"], 2 * p + g)
                for t in range(T):
                    a = g * N + t * P
                    to = ps_upd[:, t * D:(t + 1) * D]
                    pe.matmul(to, xnT[:, a:a + P], Wu_sb[:, :], start=True, stop=False)
                    pe.matmul(to, ones16[0:1, :], bias_h[:, :], start=False, stop=False)
                    last = pe.matmul(to, ones16[0:1, :], bias_l[:, :], start=False, stop=True)
                last.then_inc(s["upd_ps"], 1)

            def rank(p):
                pe.wait_ge(s["member"], p + 1)
                pe.matmul(ps_rank[:, :], earlier[:, :], member[:, :, :].rearrange("p t e -> p (t e)"), start=True, stop=False)
                for k in range(1, Q):
                    pe.matmul(ps_rank[:, k * E:Q * E], ones16[:, :], member[:, 0:Q - k, :].rearrange("p t e -> p (t e)"),
                              start=False, stop=(k == Q - 1))
                for t in range(Q):
                    last = pe.matmul(ps_placed[:, :], ones16[:, :], member[:, t, :], start=(t == 0), stop=(t == Q - 1))
                last.then_inc(s["rank_ps"], 1)

            def neighbours(p, g, q):
                pe.wait_ge(s["msg_low"], 2 * p + g + 1)
                pe.wait_ge(s["adj16"], 2 * p + g + 1)
                if later(p, 1):
                    pe.wait_ge(s["summed"], p)
                for j in range(T):
                    to = ps_sum[g][:, j * D:(j + 1) * D]
                    for i in range(T):
                        pe.matmul(to, adj16[q][g][:, i, j * P:(j + 1) * P], msgh[q][:, g * T + i, :], start=(i == 0), stop=False)
                        pe.matmul(to, adj16[q][g][:, i, j * P:(j + 1) * P], msgl[q][:, g * T + i, :],
                                  start=False, stop=(i == T - 1))

            def degrees(p, q):
                for g in range(2):
                    for j in range(T):
                        for i in range(T):
                            last = pe.matmul(ps_deg[:, g * T + j:g * T + j + 1], adj16[q][g][:, i, j * P:(j + 1) * P],
                                             ones16[:, 0:1], start=(i == 0), stop=(i == T - 1))
                last.then_inc(s["sum_ps"], 1)

            def turn_gains():
                pe.wait_ge(s["gains_in"], 16 * len(gain_loads))
                pe.wait_ge(s["upd"], B)
                pe.transpose(ps_gains[:, 0:2 * E], gb_rows[:, :], ident[0:2 * E, 0:2 * E])
                pe.transpose(ps_gains[:, 2 * E:2 * E + E * C], b1_rows[:, :], ident[0:E * C, 0:E * C]).then_inc(s["gbT_ps"], 1)

            def offsets(first, count=2):
                if first == 0:
                    pe.wait_ge(s["b1T"], 1)
                    pe.wait_ge(s["w1_in"], 32)
                for e in range(first, first + count):
                    for c in range(C):
                        last = pe.matmul(ps_hb[:, e * C + c:e * C + c + 1], W1_raw[e // 4][:, e % 4, c * P:(c + 1) * P],
                                         offset[:, e:e + 1], start=True, stop=True)
                last.then_inc(s["hb_ps"], 1)

            def step(n, q):
                draining = isinstance(n, int) and n > H
                if has(n, 3):
                    turn_rows(n - 3, 0)
                if has(n, 1):
                    turn_nodes(n - 1, 0)
                if has(n, 3):
                    turn_rows(n - 3, 1)
                if has(n, 1):
                    messages(n - 1, 0)
                if has(n, 3):
                    if has(n, 2):
                        pe.wait_ge(s["degw"], n - 1)
                    logits(n - 3)
                    if draining:
                        offsets(4 * (n - H - 1))
                if has(n, 1):
                    turn_nodes(n - 1, 1)
                    updates(n - 1, 0)
                    messages(n - 1, 1)
                    updates(n - 1, 1)
                if has(n, 3):
                    rank(n - 3)
                if isinstance(n, int) and n == H:
                    turn_gains()
                if draining:
                    offsets(4 * (n - H - 1) + 2)
                if has(n, 1):
                    neighbours(n - 1, 0, 1 - q)
                    neighbours(n - 1, 1, 1 - q)
                    if has(n, 3):
                        pe.wait_ge(s["pos"], n - 2)
                        pe.wait_ge(s["free_row"], n - 2)
                    elif has(n, 2):
                        pe.wait_ge(s["degw"], n - 1)
                    degrees(n - 1, 1 - q)

            pair_steps(pe, step)

            pe.wait_ge(s["table"], 1)
            pe.wait_ge(s["h_bias"], 1)
            pe.wait_ge(s["upd"], B)
            pe.wait_ge(s["rowT"], B)
            pe.wait_ge(s["summed"], H)

            def expert(t):
                return pe.value_load(tile_expert[0:1, at(t)], min_val=0, max_val=E - 1)

            def turn(t, q):
                loaded(pe, "tin", t, q)
                if later(t, 2):
                    pe.wait_ge(s["tT"], t - 1)
                for part in range(2):
                    for u in range(SUB):
                        at_ = part * ROWS + u * P
                        last = pe.transpose(ps_tT[q][:, at_:at_ + P], tin16[q][:, u, part * D:(part + 1) * D], ident16[:, :])
                last.then_inc(s["tT_ps"], 1)

            def hidden(t, q, e):
                pe.wait_ge(s["tT"], t + 1)
                if not later(t, 1):
                    pe.wait_ge(s["w1l"], E)
                for c in range(C):
                    if c % 2 == 0 and later(t, 1):
                        pe.wait_ge(s["gel"], 2 * t + c // 2 - 1)
                    w = bass.ds(e * HID + c * P, P)
                    high, low = tT[q][:, 0, :], tT[q][:, 1, :]
                    pe.matmul(ps_h[c], W1h[:, w], high, start=True, stop=False)
                    pe.matmul(ps_h[c], W1h[:, w], low, start=False, stop=False)
                    pe.matmul(ps_h[c], W1l[:, w], high, start=False, stop=True).then_inc(s["h_ps"], 1)

            def output(t, q, e):
                if later(t, 2):
                    pe.wait_ge(s["y"], t - 1)
                if not later(t, 1):
                    pe.wait_ge(s["w2l"], 1)
                for u in range(SUB):
                    to = ps_y[q][:, u * D:(u + 1) * D]
                    for c in range(C):
                        if u == 0 and c % 2 == 0:
                            pe.wait_ge(s["gell"], 2 * t + c // 2 + 1)
                        w = bass.ds(e * C * D + c * D, D)
                        gh = gelh[q][:, c, u * P:(u + 1) * P]
                        gl = gell[q][:, c, u * P:(u + 1) * P]
                        pe.matmul(to, gh, W2h[:, w], start=(c == 0), stop=False)
                        pe.matmul(to, gh, W2l[:, w], start=False, stop=False)
                        last = pe.matmul(to, gl, W2h[:, w], start=False, stop=(c == C - 1))
                last.then_inc(s["y_ps"], 1)

            def tile_step(n, q):
                if has(n, -1, TILES):
                    turn(n + 1, 1 - q)
                if has(n, 0, TILES):
                    hidden(n, q, expert(n))
                if has(n, 1, TILES):
                    output(n - 1, 1 - q, expert(n - 1))

            turn(0, 0)
            tile_steps(pe, tile_step)

        @block.scalar
        def _(act):
            act.dma_start(Wm_sb[:, :], W_msg).then_inc(s["msg_w_in"], 16)
            for dst, src in const_loads:
                act.dma_start(dst, src).then_inc(s["const_in"], 16)
            act.wait_ge(s["const_pool"], 1)
            act.activation(warm[:, :], eps_col[:, :], ACT.Sqrt)

            def nodes(p, g):
                act.wait_ge(s["shiftA"], p + 1)
                if later(p, 1):
                    act.wait_ge(s["xnT_ps"], 2 * p + g - 1)
                for t in range(g * T, (g + 1) * T):
                    last = act.activation(xn[:, t, :], block_x2(p, t), ACT.Identity, bias=shiftA[:, t:t + 1],
                                          scale=rs["A"][:, t:t + 1])
                last.then_inc(s["xn"], 1)

            def turned_rows(p, g):
                act.wait_ge(s["rowT_ps"], 2 * p + g + 1)
                if g == 0 and later(p, 1):
                    act.wait_ge(s["logit_ps"], p)
                act.activation(rowT[:, :, g * N:(g + 1) * N], ps_rowT[:, :].bitcast(fp16).rearrange("p (a n) -> p a n", a=2), ACT.Copy)\
                   .then_inc(s["rowT"], 1)

            def turned_nodes(p, g):
                act.wait_ge(s["xnT_ps"], 2 * p + g + 1)
                if g == 0 and later(p, 1):
                    act.wait_ge(s["upd_ps"], 2 * p)
                act.activation(xnT[:, g * N:(g + 1) * N], ps_xnT[:, :], ACT.Copy).then_inc(s["xnT"], 1)

            def convert(p, g, q):
                act.wait_ge(s[f"adj_in{g}"], 16 * (p + 1))
                if later(p, 2):
                    act.wait_ge(s["sum_ps"], p - 1)
                act.activation(adj16[q][g][:, :, :], adj_int[g][:, :, :], ACT.Copy).then_inc(s["adj16"], 1)

            def root(p, w):
                act.wait_ge(s[f"dvar{w}"], p + 1)
                if later(p, 1):
                    act.wait_ge(s[f"rs{w}"], p)
                act.activation(sd[w][:, :], dvar[w][:, :], ACT.Sqrt, scale=1.0 / D, bias=eps_col[:, :]).then_inc(s[f"sd{w}"], 1)

            def root2(p, q):
                act.wait_ge(s["dvar2"], p + 1)
                act.activation(sd2[q][:, :], dvar2[:, :], ACT.Sqrt, scale=1.0 / D, bias=eps_col[:, :]).then_inc(s["sd2"], 1)

            def high_messages(p, g, q):
                part = slice(g * T, (g + 1) * T)
                act.wait_ge(s["msg_ps"], 2 * p + g + 1)
                act.activation(msgh[q][:, part, :], ps_msg[g][:, :].rearrange("p (t d) -> p t d", t=T), ACT.Copy)\
                   .then_inc(s["msg_high"], 1)

            def updates(p, g, q):
                part = slice(g * T, (g + 1) * T)
                act.wait_ge(s["upd_ps"], 2 * p + g + 1)
                if g == 0 and later(p, 2):
                    act.wait_ge(s["summed"], p - 1)
                act.activation(upd[q][:, part, :], ps_upd[:, :].rearrange("p (t d) -> p t d", t=T), ACT.Copy).then_inc(s["upd"], 1)

            def high_rows(p, q):
                for g in range(2):
                    part = slice(g * T, (g + 1) * T)
                    act.wait_ge(s["row32"], 2 * p + g + 1)
                    if g == 0 and later(p, 1):
                        act.wait_ge(s["rowT_ps"], 2 * p)
                        loaded(act, "row_copied", p - 1, 1 - q, 16 * K)
                    act.activation(parts[:, part, 0:D], row32[:, part, :], ACT.Copy).then_inc(s["row_high"], 1)

            def gains():
                act.wait_ge(s["gbT_ps"], 1)
                act.mul(gain[:, :], ps_gains[:, 0:E], WSCALE).then_inc(s["gain"], 1)
                act.activation(offset[:, :], ps_gains[:, E:2 * E], ACT.Copy).then_inc(s["offset"], 1)
                act.activation(b1T[:, :], ps_gains[:, 2 * E:2 * E + E * C], ACT.Copy).then_inc(s["b1T"], 1)

            def first_weights(half):
                if half == 0:
                    act.wait_ge(s["gain"], 1)
                    act.wait_ge(s["w1_in"], 32)
                for e in range(4 * half, 4 * half + 4):
                    act.activation(W1h[:, e * HID:(e + 1) * HID], W1_raw[e // 4][:, e % 4, :], ACT.Copy, scale=gain[:, e:e + 1])\
                       .then_inc(s["w1h"], 1)

            def step(n, q):
                filling = isinstance(n, int) and n < 3
                if has(n, 1):
                    nodes(n - 1, 0)
                    if filling:
                        nodes(n - 1, 1)
                if has(n, 3):
                    turned_rows(n - 3, 0)
                if has(n, 1):
                    turned_nodes(n - 1, 0)
                if has(n, 3):
                    turned_rows(n - 3, 1)
                if isinstance(n, int) and n == H + 1:
                    first_weights(1)
                if has(n, 1):
                    if filling:
                        turned_nodes(n - 1, 1)
                        high_messages(n - 1, 0, 1 - q)
                        convert(n - 1, 0, 1 - q)
                    else:
                        nodes(n - 1, 1)
                        high_messages(n - 1, 0, 1 - q)
                        turned_nodes(n - 1, 1)
                if has(n, 0) and not filling:
                    convert(n, 0, q)
                if has(n, 1):
                    updates(n - 1, 0, 1 - q)
                if has(n, 2) and not filling:
                    root(n - 2, "B")
                if has(n, 1):
                    high_messages(n - 1, 1, 1 - q)
                    if filling:
                        convert(n - 1, 1, 1 - q)
                if has(n, 2):
                    if filling:
                        root(n - 2, "B")
                    root2(n - 2, q)
                if has(n, 1):
                    updates(n - 1, 1, 1 - q)
                if has(n, 0):
                    if filling and n == 2:
                        convert(n, 0, q)
                    if not filling or n == 2:
                        convert(n, 1, q)
                    root(n, "A")
                if has(n, 2):
                    high_rows(n - 2, q)
                if isinstance(n, int) and n == H:
                    gains()
                    first_weights(0)

            pair_steps(act, step)


            act.wait_ge(s["w2_in"], 64)
            for i in range(4):
                last = act.mul(W2h[:, i * 2 * HID:(i + 1) * 2 * HID], W2_raw[i][:, :, :].rearrange("p a d -> p (a d)"), WSCALE)
            last.then_inc(s["w2h"], 1)
            act.wait_ge(s["free_int"], 1)
            for e in range(1, E):
                start = act.value_load(free_int[0:1, e:e + 1], min_val=e * REGION, max_val=e * REGION + NODES)
                act.dma_start(region_part(start), pad_rows[:, :, :]).then_inc(s["pads"], 16)
            act.wait_ge(s["member"], H)
            act.activation(ex[:, :], margin[:, :, :].rearrange("p b t -> p (b t)"), ACT.Exp).then_inc(s["ex"], 1)

            act.wait_ge(s["h_bias"], 1)
            act.wait_ge(s["table"], 1)

            def turned(t, q):
                act.wait_ge(s["tT_ps"], t + 1)
                if later(t, 2):
                    act.wait_ge(s["h_ps"], C * (t - 1))
                act.activation(tT[q][:, :, :].rearrange("p a r -> p (a r)"), ps_tT[q], ACT.Copy).then_inc(s["tT"], 1)

            def gelu(t, q):
                e = act.value_load(tile_expert[0:1, at(t)], min_val=0, max_val=E - 1)
                for c in range(C):
                    act.wait_ge(s["h_ps"], C * t + c + 1)
                    if c % 2 == 0 and later(t, 2):
                        act.wait_ge(s["gell"], 2 * (t - 2) + c // 2 + 1)
                    last = act.activation(gel[q][:, c, :], ps_h[c], ACT.Gelu, bias=h_bias[:, bass.ds(e * C + c, 1)],
                                          scale=1.0 / WSCALE)
                    if c % 2:
                        last.then_inc(s["gel"], 1)

            def tile_step(n, q):
                if has(n, -1, TILES):
                    turned(n + 1, 1 - q)
                if has(n, 0, TILES):
                    gelu(n, q)

            turned(0, 0)
            tile_steps(act, tile_step)

            act.wait_ge(s["weight"], 1)

            def store(p, i):
                act.wait_ge(s["total"], p + 1)
                act.dma_start(out[pair_of(p)].rearrange("g (t p) d -> p (g t) d", p=P), total[i]).then_inc(s[f"stored{i}"], 16)

            def weighted_second(p, i):
                results_loaded(act, 1, p, i)
                if later(p, 2):
                    act.wait_ge(s["total"], p - 1)
                for t in range(Q):
                    last = act.activation(second[i % 2][:, t, :], yk[i][:, 1, t, :], ACT.Copy, scale=weight[:, 1, at(p * Q + t)])
                last.then_inc(s["second"], 1)
                if later(p, 1):
                    store(p - 1, (i - 1) % 4)

            sum_steps(act, weighted_second)
            store(H - 1, 3)
            for i in range(4):
                act.wait_ge(s[f"stored{i}"], 16 * (H // 4))

        @block.vector
        def _(dve):
            def small_constants():
                dve.wait_ge(s["const_pool"], 1)
                dve.wait_ge(s["const_in"], 16 * len(const_loads))
                dve.tensor_copy(Wrh[:, :], Wr_sb[:, :]).then_inc(s["wr_high"], 1)
                dve.tensor_copy(bias_h[:, :], bias_row[:, :]).then_inc(s["bias_high"], 1)
                dve.wait_ge(s["wr_high"], 1)
                dve.tensor_tensor(Wrl[:, :], Wr_sb[:, :], Wrh[:, :], ALU.subtract).then_inc(s["wr_low"], 1)
                dve.wait_ge(s["bias_high"], 1)
                dve.tensor_tensor(bias_l[:, :], bias_row[:, :], bias_h[:, :], ALU.subtract).then_inc(s["bias_low"], 1)

            def wide(a, n=E):
                return a.unsqueeze(2).to_broadcast([P, Q, n])

            def block_stats(p, w, q, blocks):
                dve.wait_ge(s["const_id0"], 1)
                if w == "B":
                    dve.wait_ge(s["x2"], 2 * p + 2)
                else:
                    loaded(dve, "x_in", p, q)
                for t in blocks:
                    last = dve.bn_stats(stats[w][:, t, :], block_x2(p, t))
                last.then_inc(s[f"bn{w}"], 1)

            def both_halves(p, w, waits):
                dve.wait_ge(s[f"bn{w}"], waits)
                dve.tensor_tensor(gap[w][:, :], stats[w][:, :, 1], stats[w][:, :, 4], ALU.subtract)
                dve.tensor_tensor(spread[w][:, :], stats[w][:, :, 2], stats[w][:, :, 5], ALU.add)
                dve.tensor_tensor(mean2[w][:, :], stats[w][:, :, 1], stats[w][:, :, 4], ALU.add).then_inc(s[f"level{w}"], 1)

            def gap_square(p, w):
                dve.wait_ge(s[f"level{w}"], p + 1)
                dve.scalar_tensor_tensor(gap_sq[w][:, :], gap[w][:, :], D / 4.0, gap[w][:, :], ALU.mult, ALU.mult)\
                   .then_inc(s[f"gap_sq{w}"], 1)

            def variance(p, w):
                dve.wait_ge(s[f"gap_sq{w}"], p + 1)
                dve.tensor_tensor(dvar[w][:, :], gap_sq[w][:, :], spread[w][:, :], ALU.add).then_inc(s[f"dvar{w}"], 1)

            def inverse(p, w):
                dve.wait_ge(s[f"sd{w}"], p + 1)
                dve.reciprocal(rs[w][:, :], sd[w][:, :]).then_inc(s[f"rs{w}"], 1)

            def shift(p):
                dve.wait_ge(s["rsA"], p + 1)
                dve.scalar_tensor_tensor(shiftA[:, :], mean2["A"][:, :], -0.5, rs["A"][:, :], ALU.mult, ALU.mult)\
                   .then_inc(s["shiftA"], 1)

            def low_rows(p, g):
                part = slice(g * T, (g + 1) * T)
                dve.wait_ge(s["row_high"], 2 * p + g + 1)
                dve.tensor_tensor(parts[:, part, D:2 * D], row32[:, part, :], parts[:, part, 0:D], ALU.subtract)\
                   .then_inc(s["row_low"], 1)

            def result_places(p, q):
                if later(p, 2):
                    dve.wait_ge(s[f"scattered{q}"], scattered(p, q))
                dve.tensor_copy(row[q][:, :, :, D:RW].bitcast(i32).rearrange("p k t a -> p k (t a)"),
                                result_rows[:, at(p), :, :].rearrange("p o k t -> p (o k) t"))

            def degree_floor(p):
                dve.wait_ge(s["sum_ps"], p + 1)
                dve.tensor_scalar(degm[:, :], ps_deg[:, :], 1.0, None, ALU.max).then_inc(s["degm"], 1)

            def degree_inverse(p):
                dve.wait_ge(s["degm"], p + 1)
                dve.reciprocal(degr[:, :], degm[:, :]).then_inc(s["degr"], 1)

            def degree_weight(p):
                dve.wait_ge(s["degr"], p + 1)
                dve.scalar_tensor_tensor(degw[:, :], ps_deg[:, :], 0.0, degr[:, :], ALU.is_gt, ALU.mult).then_inc(s["degw"], 1)

            def add_messages(p, q):
                dve.wait_ge(s["degw"], p + 1)
                dve.wait_ge(s["upd"], 2 * p + 2)
                for t in range(Q):
                    last = dve.scalar_tensor_tensor(summed[:, t, :], ps_sum[t // T][:, (t % T) * D:(t % T + 1) * D], degw[:, t:t + 1],
                                                    upd[q][:, t, :], ALU.mult, ALU.add)
                last.then_inc(s["summed"], 1)

            def residual(p):
                dve.wait_ge(s["summed"], p + 1)
                for g in range(2):
                    dve.scalar_tensor_tensor(pair_x2(p, g), summed[:, g * T:(g + 1) * T, :], 0.0, pair_x2(p, g), ALU.max, ALU.add)\
                       .then_inc(s["x2"], 1)

            def biased_logits_a(p, q):
                dve.wait_ge(s["logit_ps"], p + 1)
                dve.tensor_tensor(lg0[:, :, :], ps_logit[:, :].rearrange("p (t e) -> p t e", t=Q), wide(sd2[q][:, :]), ALU.mult)\
                   .then_inc(s["lg0"], 1)

            def biased_logits_b(p):
                dve.wait_ge(s["lg0"], p + 1)
                dve.tensor_tensor(lg[:, :, :], lg0[:, :, :], br_all[:, :].unsqueeze(1).to_broadcast([P, Q, E]), ALU.add)\
                   .then_inc(s["lg"], 1)

            def largest(p, k):
                logits, ready = ((lg, "lg"), (lg2, "lg2"))[k]
                dve.wait_ge(s[ready], p + 1)
                dve.tensor_reduce(top[:, k, :], logits[:, :, :], AX, ALU.max).then_inc(s[f"top{k + 1}"], 1)

            def hits(p, k):
                dve.wait_ge(s[f"top{k + 1}"], p + 1)
                dve.tensor_tensor(hit[k][:, :, :], (lg, lg2)[k][:, :, :], wide(top[:, k, :]), ALU.is_equal).then_inc(s[f"hit{k + 1}"], 1)

            def keys(p, k):
                dve.wait_ge(s[f"hit{k + 1}"], p + 1)
                dve.scalar_tensor_tensor(key[k][:, :, :], hit[k][:, :, :], -float(E), expert_no8[:, :, :], ALU.mult, ALU.add)\
                   .then_inc(s[f"key{k + 1}"], 1)

            def choose(p, k):
                dve.wait_ge(s[f"key{k + 1}"], p + 1)
                dve.tensor_reduce(chosen[k][:, :], key[k][:, :, :], AX, ALU.min).then_inc(s[f"chosen{k + 1}"], 1)

            def mark(p, k):
                dve.wait_ge(s[f"chosen{k + 1}"], p + 1)
                dve.tensor_tensor(onehot[:, k, :, :], expert_no[:, :, :], wide(chosen[k][:, :]), ALU.is_equal)\
                   .then_inc(s[f"onehot{k + 1}"], 1)

            def without_first(p):
                dve.wait_ge(s["onehot1"], p + 1)
                dve.scalar_tensor_tensor(lg2[:, :, :], onehot[:, 0, :, :], -FAR, lg[:, :, :], ALU.mult, ALU.add)\
                   .then_inc(s["lg2"], 1)

            def members(p):
                dve.tensor_tensor(margin[:, at(p), :].rearrange("p o t -> p (o t)"), top[:, 1, :], top[:, 0, :], ALU.subtract)
                dve.wait_ge(s["onehot2"], p + 1)
                dve.tensor_tensor(member[:, :, :], onehot[:, 0, :, :], onehot[:, 1, :, :], ALU.add).then_inc(s["member"], 1)

            def low_messages(p, g, q):
                part = slice(g * T, (g + 1) * T)
                dve.wait_ge(s["msg_high"], 2 * p + g + 1)
                dve.tensor_tensor(msgl[q][:, part, :], ps_msg[g][:, :].rearrange("p (t d) -> p t d", t=T), msgh[q][:, part, :],
                                  ALU.subtract).then_inc(s["msg_low"], 1)

            def inner_a(p):
                dve.wait_ge(s["rsB"], p + 1)
                dve.tensor_tensor(half_out[:, :], dvar["B"][:, :], rs["B"][:, :], ALU.mult).then_inc(s["half_out"], 1)

            def inner_b(p):
                dve.wait_ge(s["half_out"], p + 1)
                dve.tensor_tensor(dvar2[:, :], half_out[:, :], rs["B"][:, :], ALU.mult).then_inc(s["dvar2"], 1)

            def places(p):
                dve.wait_ge(s["rank_ps"], p + 1)
                dve.tensor_copy(before[:, at(p), :].rearrange("a o e -> a (o e)"), free_row[0:1, :])
                dve.tensor_tensor(pos[:, :, :], ps_rank[:, :].rearrange("p (t e) -> p t e", t=Q),
                                  free_row[:, :].unsqueeze(1).to_broadcast([P, Q, E]), ALU.add).then_inc(s["pos"], 1)

            def pick(p):
                dve.wait_ge(s["pos"], p + 1)
                dve.tensor_tensor(free_row[:, :], free_row[:, :], ps_placed[:, :], ALU.add).then_inc(s["free_row"], 1)
                dve.tensor_tensor(picked[:, :, :, :], onehot[:, :, :, :],
                                  pos[:, :, :].unsqueeze(1).to_broadcast([P, K, Q, E]), ALU.mult).then_inc(s["picked"], 1)

            def destinations(p, q):
                dve.wait_ge(s["picked"], p + 1)
                with nc.allow_low_precision(reason="summed in float32: one whole number under 2 ** 24, and zeros"):
                    dve.tensor_reduce(dest[q][:, :, :], picked[:, :, :, :], AX, ALU.add).then_inc(s["dest"], 1)

            def rows_a(p, q):
                dve.wait_ge(s["sd2"], p + 1)
                dve.reciprocal(rs2[:, :], sd2[q][:, :]).then_inc(s["rs2"], 1)
                dve.tensor_scalar(meanB[:, :], mean2["B"][:, :], 0.5, None, ALU.mult)

            def rows_b(p):
                dve.wait_ge(s["rs2"], p + 1)
                dve.tensor_tensor(rsBoth[:, :], rs["B"][:, :], rs2[:, :], ALU.mult).then_inc(s["rsBoth"], 1)

            def rows_c(p):
                dve.wait_ge(s["rsBoth"], p + 1)
                for g in range(2):
                    for t in range(g * T, (g + 1) * T):
                        last = dve.tensor_scalar(row32[:, t, :], block_x2(p, t), meanB[:, t:t + 1], rsBoth[:, t:t + 1],
                                                 ALU.subtract, ALU.mult)
                    last.then_inc(s["row32"], 1)

            def first_weights(a, b):
                dve.wait_ge(s["w1h"], b)
                for e in range(a, b):
                    dve.scalar_tensor_tensor(W1l[:, e * HID:(e + 1) * HID], W1_raw[e // 4][:, e % 4, :], gain[:, e:e + 1],
                                             W1h[:, e * HID:(e + 1) * HID], ALU.mult, ALU.subtract).then_inc(s["w1l"], 1)

            def step(n, q):
                ahead, first, second, third = has(n, 0), has(n, 1), has(n, 2), has(n, 3)
                filling = isinstance(n, int) and n < 3
                if first:
                    inverse(n - 1, "A")
                if first:
                    shift(n - 1)
                if third:
                    low_rows(n - 3, 0)
                if isinstance(n, int) and n == 1:
                    small_constants()
                if third:
                    low_rows(n - 3, 1)
                if isinstance(n, int) and n == H + 2:
                    first_weights(0, 6)
                if second:
                    degree_floor(n - 2)
                if second:
                    degree_inverse(n - 2)
                if ahead:
                    block_stats(n, "A", q, (0, 1))
                if second:
                    degree_weight(n - 2)
                if ahead:
                    block_stats(n, "A", q, (2,))
                if second:
                    add_messages(n - 2, q)
                if ahead:
                    block_stats(n, "A", q, (3,))
                if second:
                    residual(n - 2)
                if third:
                    biased_logits_a(n - 3, 1 - q)
                if second:
                    block_stats(n - 2, "B", q, (0, 1))
                if third:
                    biased_logits_b(n - 3)
                if second:
                    block_stats(n - 2, "B", q, (2, 3))
                if third:
                    largest(n - 3, 0)
                if second:
                    block_stats(n - 2, "B", q, (4, 5))
                if third:
                    hits(n - 3, 0)
                if second:
                    block_stats(n - 2, "B", q, (6, 7))
                if third:
                    keys(n - 3, 0)
                if second:
                    both_halves(n - 2, "B", 4 * (n - 2) + 4)
                if third:
                    choose(n - 3, 0)
                if second:
                    gap_square(n - 2, "B")
                if third:
                    mark(n - 3, 0)
                if second:
                    variance(n - 2, "B")
                if third:
                    without_first(n - 3)
                if first:
                    low_messages(n - 1, 0, 1 - q)
                if third:
                    largest(n - 3, 1)
                if first and filling:
                    low_messages(n - 1, 1, 1 - q)
                if second:
                    inverse(n - 2, "B")
                if third:
                    hits(n - 3, 1)
                if second:
                    inner_a(n - 2)
                if third:
                    keys(n - 3, 1)
                if second:
                    inner_b(n - 2)
                if third:
                    choose(n - 3, 1)
                if first and not filling:
                    low_messages(n - 1, 1, 1 - q)
                if third:
                    mark(n - 3, 1)
                if third:
                    members(n - 3)
                if ahead:
                    block_stats(n, "A", q, (4, 5, 6, 7))
                if second:
                    rows_a(n - 2, q)
                if ahead:
                    both_halves(n, "A", 4 * n + 4)
                if second:
                    rows_b(n - 2)
                if ahead:
                    gap_square(n, "A")
                if third:
                    result_places(n - 3, 1 - q)
                    places(n - 3)
                if ahead:
                    variance(n, "A")
                if third:
                    pick(n - 3)
                if second:
                    rows_c(n - 2)
                if third:
                    destinations(n - 3, 1 - q)

            pair_steps(dve, step)

            dve.wait_ge(s["free_row"], H)
            dve.tensor_copy(free_int[:, :], free_row[0:1, :]).then_inc(s["free_int"], 1)
            dve.scalar_tensor_tensor(count[:, :], expert_no[0:1, 0, :], -float(REGION), free_row[0:1, :], ALU.mult, ALU.add)\
               .then_inc(s["cnt"], 1)
            dve.wait_ge(s["cnt"], 1)
            dve.tensor_tensor(over[:, :, :], count[:, :].unsqueeze(2).to_broadcast([1, E, NODES // ROWS]), steps32[:, :, :], ALU.is_gt)\
               .then_inc(s["over"], 1)
            dve.wait_ge(s["over"], 1)
            dve.tensor_reduce(ntile[:, :], over[:, :, :], AX, ALU.add).then_inc(s["ntile"], 1)
            dve.wait_ge(s["ntile"], 1)
            dve.tensor_tensor(prod[:, :, :], ntile[:, :].unsqueeze(1).to_broadcast([1, E, E]), upto[:, :, :], ALU.mult)\
               .then_inc(s["prod"], 1)
            dve.tensor_scalar(jump[:, :], ntile[:, :], -float(ROWS), float(REGION), ALU.mult, ALU.add).then_inc(s["jump"], 1)
            dve.wait_ge(s["prod"], 1)
            dve.tensor_reduce(tile_end[:, :], prod[:, :, :], AX, ALU.add).then_inc(s["tile_end"], 1)
            dve.wait_ge(s["tile_end"], 1)
            dve.tensor_tensor(past[:, :, :], tile_no[:, :, :], tile_end[:, :].unsqueeze(1).to_broadcast([1, TILES, E]), ALU.is_ge)\
               .then_inc(s["past"], 1)
            dve.wait_ge(s["past"], 1)
            dve.wait_ge(s["jump"], 1)
            dve.tensor_reduce(t_expert[:, :], past[:, :, :], AX, ALU.add).then_inc(s["t_expert"], 1)
            dve.tensor_tensor(moved[:, :, :], past[:, :, :], jump[:, :].unsqueeze(1).to_broadcast([1, TILES, E]), ALU.mult)\
               .then_inc(s["moved"], 1)
            dve.wait_ge(s["moved"], 1)
            dve.tensor_reduce(t_row[:, :], moved[:, :, :], AX, ALU.add).then_inc(s["t_row0"], 1)
            dve.wait_ge(s["t_row0"], 1)
            dve.scalar_tensor_tensor(t_row[:, :], tile_no[:, :, 0], float(ROWS), t_row[:, :], ALU.mult, ALU.add)\
               .then_inc(s["t_row1"], 1)
            dve.wait_ge(s["t_row1"], 1)
            dve.tensor_scalar(tile_expert[:, :], t_expert[:, :], float(E - 1), None, ALU.min)
            dve.tensor_scalar(tile_row[:, :], t_row[:, :], float(SPARE), None, ALU.min).then_inc(s["table"], 1)

            dve.tensor_tensor(own[:, :, :], expert_no[0:1, 0:EARLY, :], t_expert[:, 0:EARLY].unsqueeze(2).to_broadcast([1, EARLY, E]),
                              ALU.is_equal)
            dve.tensor_scalar(pads_part[:, :], t_expert[:, 0:EARLY], 1.0 / E, 1.0, ALU.add, ALU.min)
            dve.tensor_scalar(limit[:, :], t_row[:, 0:EARLY], float(ROWS), None, ALU.add).then_inc(s["own"], 1)
            dve.wait_ge(s["own"], 1)
            dve.tensor_tensor(short[:, :, :, :], before[:, 1:H, :].unsqueeze(1).to_broadcast([1, EARLY, H - 1, E]),
                              limit[:, :].unsqueeze(2).unsqueeze(3).to_broadcast([1, EARLY, H - 1, E]), ALU.is_lt).then_inc(s["short"], 1)
            dve.wait_ge(s["short"], 1)
            dve.tensor_tensor(own_short[:, :, :, :], short[:, :, :, :], own[:, :, :].unsqueeze(2).to_broadcast([1, EARLY, H - 1, E]),
                              ALU.mult).then_inc(s["own_short"], 1)
            dve.wait_ge(s["own_short"], 1)
            dve.tensor_reduce(more[:, :, :], own_short[:, :, :, :], AX, ALU.add).then_inc(s["more"], 1)
            dve.wait_ge(s["more"], 1)
            dve.tensor_reduce(needed[:, 0, :], more[:, :, 1:H - 1:2], AX, ALU.add)
            dve.tensor_reduce(needed[:, 1, :], more[:, :, 0:H - 1:2], AX, ALU.add).then_inc(s["needed"], 1)
            dve.wait_ge(s["needed"], 1)
            dve.tensor_scalar(needed_pads[:, :], pads_part[:, :], 16.0 * E, None, ALU.mult)
            dve.tensor_scalar(needed_rows[:, 0, :], needed[:, 0, :], 16.0 * K * Q, 16.0 * K * Q, ALU.mult, ALU.add)
            dve.tensor_scalar(needed_rows[:, 1, :], needed[:, 1, :], 1.0, 16.0 * K * Q, ALU.max, ALU.mult).then_inc(s["needed_rows"], 1)

            dve.wait_ge(s["hb_ps"], E // 2)
            dve.tensor_tensor(h_bias[:, :], ps_hb[:, :], b1T[:, :], ALU.add).then_inc(s["h_bias"], 1)
            first_weights(6, E)
            dve.wait_ge(s["w2h"], 1)
            for i in range(4):
                part = slice(i * 2 * HID, (i + 1) * 2 * HID)
                last = dve.scalar_tensor_tensor(W2l[:, part], W2_raw[i][:, :, :].rearrange("p a d -> p (a d)"), WSCALE, W2h[:, part],
                                                ALU.mult, ALU.subtract)
            last.then_inc(s["w2l"], 1)
            dve.wait_ge(s["ex"], 1)
            dve.tensor_scalar(ex1[:, :], ex[:, :], 1.0, None, ALU.add).then_inc(s["ex1"], 1)
            dve.wait_ge(s["ex1"], 1)
            dve.reciprocal(weight[:, 0, :], ex1[:, :]).then_inc(s["wt0"], 1)
            dve.wait_ge(s["wt0"], 1)
            dve.tensor_tensor(weight[:, 1, :], weight[:, 0, :], ex[:, :], ALU.mult).then_inc(s["weight"], 1)

            def note(t, q):
                loaded(dve, "tin", t, q)
                dve.tensor_copy(result_row[:, at(t), :].rearrange("p o u -> p (o u)"),
                                tin[q][:, :, D:RW].bitcast(u32).rearrange("p u a -> p (u a)")).then_inc(s["result_row"], 1)

            def split(t, q):
                for half in range(2):
                    part = slice(half * (C // 2), (half + 1) * (C // 2))
                    dve.wait_ge(s["gel"], 2 * t + half + 1)
                    dve.tensor_copy(gelh[q][:, part, :], gel[q][:, part, :]).then_inc(s["gelh"], 1)
                    dve.wait_ge(s["gelh"], 2 * t + half + 1)
                    dve.tensor_tensor(gell[q][:, part, :], gel[q][:, part, :], gelh[q][:, part, :], ALU.subtract)\
                       .then_inc(s["gell"], 1)

            def finish(t, q):
                e = dve.value_load(tile_expert[0:1, at(t)], min_val=0, max_val=E - 1)
                dve.wait_ge(s["y_ps"], t + 1)
                if later(t, 2):
                    dve.wait_ge(s[f"sent{q}"], 16 * SUB * (t // 2) if isinstance(t, int) else 8 * SUB * (t - q))
                dve.tensor_copy(send_to[q][:, :], result_row[:, at(t), :].rearrange("p o u -> p (o u)"))
                dve.scalar_tensor_tensor(y[q][:, :, :], ps_y[q][:, 0:SUB * D].rearrange("p (u d) -> p u d", u=SUB), 1.0 / WSCALE,
                                         b2_all[:, bass.ds(e, 1), :].to_broadcast([P, SUB, D]), ALU.mult, ALU.add)\
                   .then_inc(s["y"], 1)

            def tile_step(n, q):
                if has(n, 2, TILES):
                    finish(n - 2, q)
                if has(n, -1, TILES):
                    note(n + 1, 1 - q)
                if has(n, 0, TILES):
                    split(n, q)

            dve.wait_ge(s["gains_in"], 16 * len(gain_loads))
            note(0, 0)
            tile_steps(dve, tile_step)

            def add(p, i):
                dve.wait_ge(s["first"], p + 1)
                dve.wait_ge(s["second"], p + 1)
                if later(p, 4):
                    dve.wait_ge(s[f"stored{i}"], 16 * (p // 4) if isinstance(p, int) else 4 * (p - i))
                dve.tensor_tensor(total[i], first[i % 2][:, :, :], second[i % 2], ALU.add).then_inc(s["total"], 1)

            def combine(p, i):
                q = i % 2
                results_loaded(dve, 0, p, i)
                if later(p, 2):
                    dve.wait_ge(s["total"], p - 1)
                for t in range(Q):
                    last = dve.scalar_tensor_tensor(first[q][:, t, :], yk[i][:, 0, t, :], weight[:, 0, at(p * Q + t)], block_x2(p, t),
                                                    ALU.mult, ALU.add)
                last.then_inc(s["first"], 1)
                if later(p, 1):
                    add(p - 1, (i - 1) % 4)

            dve.wait_ge(s["weight"], 1)
            sum_steps(dve, combine)
            add(H - 1, 3)


_INS = ["x", "adj", "L0_gnn_W_msg", "L0_gnn_W_upd", "L0_gnn_bias", "L0_ffn_Wr", "L0_ffn_br", "L0_ffn_ln_g", "L0_ffn_ln_b",
        "L0_ffn_W1", "L0_ffn_b1", "L0_ffn_W2", "L0_ffn_b2"]


def kernel(**inputs):
    import numpy as _np
    import concourse.bacc as _bacc
    from concourse import mybir as _mybir
    from concourse.bass_utils import run_bass_kernel_spmd as _run

    nc = _bacc.Bacc("TRN2", target_bir_lowering=False, num_devices=1)
    arrays, args = {}, []
    for name in _INS:
        a = _np.ascontiguousarray(inputs[name])
        arrays[f"in_{name}_dram"] = a
        args.append(nc.dram_tensor(f"in_{name}_dram", a.shape, _mybir.dt.from_np(a.dtype), kind="ExternalInput").ap())
    args.append(nc.dram_tensor("out_dram", (16, 512, 128), _mybir.dt.float32, kind="ExternalOutput").ap())
    graph_then_experts_kernel(nc, *args)
    r = _run(nc, [arrays], core_ids=[0])
    return r.results[0]["out_dram"]
```
